# Optimizing a Trainium2 kernel written in Bass

```python
import numpy as np
import jax
import jax.numpy as jnp

def _softmax(x, axis=-1):
    return jax.nn.softmax(x, axis=axis)

def _gelu(x):
    return jax.nn.gelu(x, approximate=True)

def _silu(x):
    return jax.nn.silu(x)

def _sigmoid(x):
    return jax.nn.sigmoid(x)

def _layernorm(x, axis=-1, eps=1e-05):
    m = jnp.mean(x, axis=axis, keepdims=True)
    v = jnp.var(x, axis=axis, keepdims=True)
    return (x - m) / jnp.sqrt(v + eps)

def _scatter_add(tgt, idx, src, axis=0):
    return tgt.at[idx].add(src)

def _segment_sum(src, seg, n):
    return jax.ops.segment_sum(src, seg, n)
kernel_name = 'mk_flamingo_gated_d1_seqx_r4_1fc376'

def setup_inputs(seed: int=0):
    np.random.seed(seed)
    _w = jnp.asarray

    def _rec_inputs():
        import jax
        import jax.numpy as jnp
        _rk = jax.random.key(seed)
        x = -0.0002928 + 1 * jax.random.normal(jax.random.fold_in(_rk, 1), (16, 128, 1024), jnp.float32)
        _lenS = 128 - jax.random.randint(jax.random.fold_in(_rk, 7), (16,), 0, max(1, 128 // 4) + 1, jnp.int32)
        _lenS2 = 128 - jax.random.randint(jax.random.fold_in(_rk, 8), (16,), 0, max(1, 128 // 4) + 1, jnp.int32)
        _ctx_4096P = jax.random.normal(jax.random.fold_in(_rk, 11), (16, 16, 1024), jnp.float32)
        _ctx_4096c = jax.random.dirichlet(jax.random.fold_in(_rk, 511), 0.3 * jnp.ones((16,), jnp.float32), (16, 128))
        _ctx_4096t = jnp.einsum('bsk,bkd->bsd', _ctx_4096c, _ctx_4096P)
        _ctx_4096t = _ctx_4096t * jax.lax.rsqrt(jnp.mean(jnp.square(_ctx_4096t)) + 1e-12) * 0.953939
        ctx_4096 = -2.8382e-05 + 0.999851 * (_ctx_4096t + 0.3 * jax.random.normal(jax.random.fold_in(_rk, 611), (16, 128, 1024), jnp.float32))
        _validS = jnp.arange(128)[None, :] < _lenS[:, None]
        _validS2 = jnp.arange(128)[None, :] < _lenS2[:, None]
        _causal = jnp.tril(jnp.ones((128, 128), dtype=bool))
        mask_1x1xSxS2_ff0 = jnp.where(jnp.ones((1, 1, 128, 128), dtype=bool), 0.0, -1000000000.0).astype(jnp.float32)
        _g = jax.random.normal(jax.random.fold_in(_rk, 9001), (2, 1), jnp.float32)
        _g = jnp.sign(_g) * jnp.maximum(jnp.abs(_g), 1.0) + (_g == 0) * 1.0
        g_xattn = _g[0]
        g_ffn = _g[1]
        return (x, ctx_4096, mask_1x1xSxS2_ff0, g_xattn, g_ffn)
    x, ctx_4096, mask_1x1xSxS2_ff0, g_xattn, g_ffn = _rec_inputs()

    def _L0_xattn_setup():
        import jax, jax.numpy as jnp
        import numpy as np
        NUM_HEADS = 32
        NUM_KV_HEADS = 8
        HEAD_DIM = 128
        HIDDEN = 1024
        EPS = 1e-05

        def rmsnorm(x, w, eps=EPS):
            xf = x.astype(jnp.float32)
            var = jnp.mean(xf * xf, axis=-1, keepdims=True)
            return w * (xf * jax.lax.rsqrt(var + eps)).astype(x.dtype)
        key = jax.random.key(seed)
        ks = jax.random.split(key, 10)
        B, Q, KV = (1, 256, 1601)
        s = 1.0 / np.sqrt(HIDDEN)
        return {'hidden_states': jax.random.normal(ks[0], (B, Q, HIDDEN), jnp.float32), 'cross_attention_states': jax.random.normal(ks[1], (B, KV, HIDDEN), jnp.float32), 'attention_mask': jnp.zeros((B, 1, Q, KV), jnp.float32), 'q_proj_w': jax.random.normal(ks[2], (NUM_HEADS * HEAD_DIM, HIDDEN), jnp.float32) * s, 'k_proj_w': jax.random.normal(ks[3], (NUM_KV_HEADS * HEAD_DIM, HIDDEN), jnp.float32) * s, 'v_proj_w': jax.random.normal(ks[4], (NUM_KV_HEADS * HEAD_DIM, HIDDEN), jnp.float32) * s, 'o_proj_w': jax.random.normal(ks[5], (HIDDEN, NUM_HEADS * HEAD_DIM), jnp.float32) * s, 'q_norm_w': jnp.ones((HEAD_DIM,), jnp.float32), 'k_norm_w': jnp.ones((HEAD_DIM,), jnp.float32)}
    _L0_xattn_all = _L0_xattn_setup()
    _L0_xattn_in = {k: v for k, v in _L0_xattn_all.items() if k in ('q_proj_w', 'k_proj_w', 'v_proj_w', 'o_proj_w', 'q_norm_w', 'k_norm_w')}
    del _L0_xattn_all

    def _L0_ffn_setup():
        import jax, jax.numpy as jnp
        import numpy as np
        BATCH, SEQ, D = (2, 512, 1024)
        K, TOPK, RANK = (64, 16, 16)
        ALPHA = 32.0
        SCALING = ALPHA / RANK
        key = jax.random.key(seed)
        k1, k2, k3, k4 = jax.random.split(key, 4)
        x = jax.random.normal(k1, (BATCH, SEQ, D), dtype=jnp.float32)
        A = jax.random.normal(k2, (K, RANK, D), dtype=jnp.float32) * 0.02
        B = jax.random.normal(k3, (K, D, RANK), dtype=jnp.float32) * 0.02
        Wr = jax.random.normal(k4, (K, D), dtype=jnp.float32) * 0.02
        return {'x': x, 'A': A, 'B': B, 'Wr': Wr}
    _L0_ffn_all = _L0_ffn_setup()
    _L0_ffn_in = {k: v for k, v in _L0_ffn_all.items() if k in ('A', 'B', 'Wr')}
    del _L0_ffn_all
    return {'x': x, 'ctx_4096': ctx_4096, 'mask_1x1xSxS2_ff0': mask_1x1xSxS2_ff0, 'g_xattn': g_xattn, 'g_ffn': g_ffn, 'L0_xattn_q_proj_w': _L0_xattn_in['q_proj_w'], 'L0_xattn_k_proj_w': _L0_xattn_in['k_proj_w'], 'L0_xattn_v_proj_w': _L0_xattn_in['v_proj_w'], 'L0_xattn_o_proj_w': _L0_xattn_in['o_proj_w'], 'L0_xattn_q_norm_w': _L0_xattn_in['q_norm_w'], 'L0_xattn_k_norm_w': _L0_xattn_in['k_norm_w'], 'L0_ffn_A': _L0_ffn_in['A'], 'L0_ffn_B': _L0_ffn_in['B'], 'L0_ffn_Wr': _L0_ffn_in['Wr']}

def reference(x, ctx_4096, mask_1x1xSxS2_ff0, g_xattn, g_ffn, L0_xattn_q_proj_w, L0_xattn_k_proj_w, L0_xattn_v_proj_w, L0_xattn_o_proj_w, L0_xattn_q_norm_w, L0_xattn_k_norm_w, L0_ffn_A, L0_ffn_B, L0_ffn_Wr):
    import jax
    import jax.numpy as jnp

    def _L0_xattn_ref(hidden_states, cross_attention_states, attention_mask, q_proj_w, k_proj_w, v_proj_w, o_proj_w, q_norm_w, k_norm_w):
        import jax, jax.numpy as jnp
        import numpy as np
        NUM_HEADS = 32
        NUM_KV_HEADS = 8
        HEAD_DIM = 128
        HIDDEN = 1024
        EPS = 1e-05

        def rmsnorm(x, w, eps=EPS):
            xf = x.astype(jnp.float32)
            var = jnp.mean(xf * xf, axis=-1, keepdims=True)
            return w * (xf * jax.lax.rsqrt(var + eps)).astype(x.dtype)
        B, Q, _ = hidden_states.shape
        KV = cross_attention_states.shape[1]
        n_rep = NUM_HEADS // NUM_KV_HEADS
        q = (hidden_states @ q_proj_w.T).reshape(B, Q, NUM_HEADS, HEAD_DIM).transpose(0, 2, 1, 3)
        k = (cross_attention_states @ k_proj_w.T).reshape(B, KV, NUM_KV_HEADS, HEAD_DIM).transpose(0, 2, 1, 3)
        v = (cross_attention_states @ v_proj_w.T).reshape(B, KV, NUM_KV_HEADS, HEAD_DIM).transpose(0, 2, 1, 3)
        q = rmsnorm(q, q_norm_w)
        k = jnp.repeat(k, n_rep, axis=1)
        v = jnp.repeat(v, n_rep, axis=1)
        k = rmsnorm(k, k_norm_w)
        scale = 1.0 / np.sqrt(HEAD_DIM)
        scores = jnp.einsum('bhqd,bhkd->bhqk', q, k) * scale + attention_mask
        attn = jax.nn.softmax(scores.astype(jnp.float32), axis=-1).astype(q.dtype)
        out = jnp.einsum('bhqk,bhkd->bhqd', attn, v)
        out = out.transpose(0, 2, 1, 3).reshape(B, Q, NUM_HEADS * HEAD_DIM)
        return out @ o_proj_w.T

    def _L0_ffn_ref(x, A, B, Wr):
        import jax, jax.numpy as jnp
        import numpy as np
        BATCH, SEQ, D = (2, 512, 1024)
        K, TOPK, RANK = (64, 16, 16)
        ALPHA = 32.0
        SCALING = ALPHA / RANK
        prefix = x.shape[:-1]
        xf = x.reshape(-1, x.shape[-1])
        N = xf.shape[0]
        scores = xf @ Wr.T
        top_vals, top_idx = jax.lax.top_k(scores, TOPK)
        gates = jax.nn.softmax(top_vals, axis=-1)
        G = jnp.zeros((N, K), xf.dtype).at[jnp.arange(N)[:, None], top_idx].set(gates)
        h = jnp.einsum('nd,krd->nkr', xf, A)
        out = jnp.einsum('nkr,kdr->nd', h * G[:, :, None], B)
        return (out * SCALING).reshape(*prefix, -1)
    x = x + jnp.tanh(g_xattn[0]) * _L0_xattn_ref(_layernorm(x, axis=-1), ctx_4096, mask_1x1xSxS2_ff0, L0_xattn_q_proj_w, L0_xattn_k_proj_w, L0_xattn_v_proj_w, L0_xattn_o_proj_w, L0_xattn_q_norm_w, L0_xattn_k_norm_w)
    x = x + jnp.tanh(g_ffn[0]) * _L0_ffn_ref(_layernorm(x, axis=-1), L0_ffn_A, L0_ffn_B, L0_ffn_Wr)
    return x

_drawn_inputs = setup_inputs


def setup_inputs(seed=0):
    import zlib

    import numpy as np

    out = dict(_drawn_inputs(seed))
    spreads = {'L0_xattn_q_norm_w': (1.0, 0.2), 'L0_xattn_k_norm_w': (1.0, 0.2)}
    factors = {'L0_ffn_Wr': 2.851}
    for name, (base, spread) in spreads.items():
        noise = np.random.default_rng([zlib.crc32(name.encode()), seed]).standard_normal(out[name].shape)
        drawn = base * np.exp(spread * noise) if base else spread * noise
        out[name] = jnp.asarray(drawn.astype(out[name].dtype))
    for name, factor in factors.items():
        out[name] = (out[name] * factor).astype(out[name].dtype)
    return out
```

```python
import concourse.bass as bass
from concourse import mybir
from contextlib import ExitStack

FP32 = mybir.dt.float32
FP32R = mybir.dt.float32r
ALU = mybir.AluOpType
ACT = mybir.ActivationFunctionType
AX = mybir.AxisListType

P = 128
S = 128
BATCHES = 16
HIDDEN = 1024
KT = HIDDEN // P
HEADS, KV_HEADS, HEAD_DIM = 32, 8, 128
GROUPS = KV_HEADS
GH = HEADS // KV_HEADS
TB = 4
BLOCKS = BATCHES // TB
TOK = TB * S
EXPERTS, RANK, TOPK = 64, 16, 16
LORA = EXPERTS * RANK
ALPHA_OVER_RANK = 32.0 / 16
EPS = 1e-5
UNIT = 1024
RING = 5
FFN_RING = 4
UPG = 10
FIRST_UNITS = 6
UPB = UPG * GROUPS
LOWEST = -3.0e38


def split_product(nc, out, pairs, first, last):
    done = None
    for i, (w_hi, w_lo, m_hi, m_lo) in enumerate(pairs):
        s, e = first and i == 0, last and i == len(pairs) - 1
        nc.tensor.matmul(out, w_hi, m_hi, start=s, stop=False)
        nc.tensor.matmul(out, w_hi, m_lo, start=False, stop=False)
        done = nc.tensor.matmul(out, w_lo, m_hi, start=False, stop=e)
    return done


class Arena:

    def __init__(self, nc, tag):
        self.nc, self.tag, self.at = nc, tag, -(-nc.sbuf_base // 64) * 64

    def put(self, name, shape, dtype=FP32, over=None):
        size = 4
        for n in shape[1:]:
            size *= n
        at = self.at if over is None else over
        t = self.nc.alloc_sbuf_tensor_at(f"{self.tag}_{name}", shape, dtype, offset=at)
        if over is None:
            self.at += -(-size // 64) * 64
        return t

    def pair(self, name, shape, raw=False):
        hi = self.put(name + "_hi", shape, FP32R)
        at = self.at
        lo = self.put(name + "_lo", shape, FP32R)
        return (hi, lo, self.put(name + "_raw", shape, FP32, over=at)) if raw else (hi, lo)


def attention_phase(nc, ctx, sem, psum, d):
    a = Arena(nc, "at")
    ring = [a.pair(f"ring{s}", [P, UNIT], raw=True) for s in range(RING)]
    cx_hi, cx_lo, cx_raw = a.pair("ctx", [P, KT, TOK], raw=True)
    xn_hi, xn_lo = a.pair("xn", [P, KT, TOK])
    x_rows = a.put("x_rows", [P, TB, HIDDEN])
    acc = a.put("acc", [P, KT, TOK])
    vn_hi, vn_lo = a.pair("v_new", [P, TB, HEAD_DIM])
    vc_hi, vc_lo = a.pair("v_cur", [P, TB, HEAD_DIM])
    k_sb = a.put("k_sb", [P, TB, HEAD_DIM])
    k_n = a.put("k_n", [P, TB, HEAD_DIM])
    kt_sb = a.put("kt_sb", [P, TB, S])
    qt = [a.put(f"qt{i}", [P, TB, S]) for i in range(2)]
    sm = a.put("scores", [P, TB, S])
    pr = a.put("probs", [P, TB, S])
    pt_hi, pt_lo = a.pair("pt", [P, TB, GH, S])
    ot_hi, ot_lo = a.pair("ot", [P, GH, TB, S])
    mask = a.put("mask", [P, S])
    ident = a.put("ident", [P, P])
    k_sq = a.put("k_squares", [P, TB, HEAD_DIM])
    nw = a.put("norm_weights", [P, 2])
    kw = a.put("k_weight", [P, 1])
    gx = a.put("gate_in", [P, 1])
    tgx = a.put("gate", [P, 1])
    eps = a.put("eps", [P, 1])
    stats = a.put("stats", [P, TB, 2, 6])
    mv = a.put("mean_var", [P, TB, 2])
    x_ln, x_seed, x_v, x_t, x_rstd = (a.put("x_" + k, [P, TB]) for k in ("ln", "seed", "v", "t", "rstd"))
    k_ss, k_ln, k_seed, k_v, k_t, k_rstd = (a.put("k_" + k, [P, TB]) for k in ("ss", "ln", "seed", "v", "t", "rstd"))
    q_ss, q_ln, q_seed, q_v, q_t, q_rstd = (a.put("q_" + k, [P, TB]) for k in ("ss", "ln", "seed", "v", "t", "rstd"))
    nmax = a.put("neg_max", [P, TB])
    rsum = a.put("row_sum", [P, TB])
    rinv = a.put("row_inv", [P, TB])
    assert a.at <= nc.sbuf_top, a.at

    bank_a, bank_b, bank_o0, bank_o1, bank_s, bank_t, bank_x, bank_v = psum
    proj = (bank_a, bank_b)

    const_in = sem("const_in")
    unit_raw = [sem(f"unit_raw{s}") for s in range(RING)]
    ctx_raw, rows_raw, acc_raw, x2t_out = sem("ctx_raw"), sem("rows_raw"), sem("acc_raw"), sem("x2t_out")
    gate_tanh, eps_set, kw_set = sem("gate_tanh"), sem("eps_set"), sem("kw_set")
    unit_hi, unit_lo, ctx_hi, ctx_lo = sem("unit_hi"), sem("unit_lo"), sem("ctx_hi"), sem("ctx_lo")
    row_stats, row_aggr, row_seed, row_norm = sem("row_stats"), sem("row_aggr"), sem("row_seed"), sem("row_norm")
    xt_done, xn_hi_done, xn_lo_done = sem("xt_done"), sem("xn_hi_done"), sem("xn_lo_done")
    kv_done, q_done, t1_done, s_done, pt_done = sem("kv_done"), sem("q_done"), sem("t1_done"), sem("s_done"), sem("pt_done")
    pv_done, o_done, kt_done = sem("pv_done"), sem("o_done"), sem("kt_done")
    k_squared, v_hi_done, k_copied, v_lo_done, k_seeded, kt_copied = (
        sem("k_squared"), sem("v_hi_done"), sem("k_copied"), sem("v_lo_done"), sem("k_seeded"), sem("kt_copied"))
    q_copied, q_squared, q_seeded = sem("q_copied"), sem("q_squared"), sem("q_seeded")
    rstd_step, k_scaled, v_moved = sem("rstd_step"), sem("k_scaled"), sem("v_moved")
    s_masked, s_max, p_exp, p_inv, p_norm = sem("s_masked"), sem("s_max"), sem("p_exp"), sem("p_inv"), sem("p_norm")
    pt_hi_done, pt_lo_done, ot_hi_done, ot_lo_done, acc_add = (
        sem("pt_hi_done"), sem("pt_lo_done"), sem("ot_hi_done"), sem("ot_lo_done"), sem("acc_add"))
    act_step = sem("act_step")
    vector_waited, pool_waited = sem("vector_waited"), sem("pool_waited")

    CONSTS = 5
    block = ctx.enter_context(nc.Block())

    ROWS, KEYS, QUERIES = 0, 1, 2

    def newton_after(b, g, item):
        return b * (5 + 25 * GROUPS) + g * 25 + 5 * (item + 1)

    SPLIT_FIRST = {0: 3, 1: 4, 2: 5, 7: 6, 8: 7, 9: 8}
    SPLIT_LATER = {i: i + 3 + FIRST_UNITS - UPG for i in range(10)}

    @block.sync
    def _(sp):
        sp.dma_start(gx[:, :], d.g_x).then_inc(const_in, 16)
        sp.dma_start(nw[:, :], d.norm_w).then_inc(const_in, 16)
        sp.dma_start(ident[:, :], d.ident).then_inc(const_in, 16)
        sp.dma_start(mask[:, :], d.mask).then_inc(const_in, 16)
        sp.dma_start(eps[:, :], d.eps).then_inc(const_in, 16)

        def unit(slot, src):
            sp.dma_start(ring[slot][2][:, :], src).then_inc(unit_raw[slot], 16)

        def first_group(b):
            unit(0, d.w_kv[0, 0])
            unit(1, d.w_kv[0, 1])
            unit(2, d.w_q[0, 0])
            unit(3, d.w_q[0, 1])
            unit(4, d.w_q[0, 2])

        def do_block(b, last):
            n = b * GROUPS
            sp.wait_ge(kv_done, n * 2 + 2)
            unit(0, d.w_q[0, 3])
            if not last:
                sp.wait_ge(xt_done, b * KT + KT)
                sp.dma_start(x_rows[:, :, :], d.x_rows[b + 1]).then_inc(rows_raw, 16)
            with sp.Fori(1, GROUPS) as g:
                n = b * GROUPS + g
                sp.wait_ge(q_done, n * 4 - 1)
                unit(1, d.w_kv[g, 0])
                unit(2, d.w_kv[g, 1])
                sp.wait_ge(q_done, n * 4)
                unit(3, d.w_q[g, 0])
                unit(4, d.w_o[g - 1, 0])
                sp.wait_ge(kv_done, n * 2 + 1)
                unit(0, d.w_q[g, 1])
                sp.wait_ge(kv_done, n * 2 + 2)
                unit(1, d.w_o[g - 1, 1])
                unit(2, d.w_q[g, 2])
                sp.wait_ge(q_done, n * 4 + 1)
                unit(3, d.w_o[g - 1, 2])
                sp.wait_ge(o_done, n * 8 - 6)
                unit(4, d.w_q[g, 3])
                sp.wait_ge(q_done, n * 4 + 2)
                unit(0, d.w_o[g - 1, 3])
            n = b * GROUPS + GROUPS
            sp.wait_ge(q_done, n * 4 - 1)
            unit(1, d.w_o[GROUPS - 1, 0])
            unit(2, d.w_o[GROUPS - 1, 1])
            sp.wait_ge(q_done, n * 4)
            unit(3, d.w_o[GROUPS - 1, 2])
            unit(4, d.w_o[GROUPS - 1, 3])
            if not last:
                sp.dma_start(cx_raw[:, :, :], d.ctx_t[b + 1]).then_inc(ctx_raw, 16)
                sp.wait_ge(o_done, n * 8 - 8)
                unit(0, d.w_kv[0, 0])
                sp.wait_ge(o_done, n * 8 - 6)
                unit(1, d.w_kv[0, 1])
                sp.wait_ge(o_done, n * 8 - 4)
                unit(2, d.w_q[0, 0])
                sp.wait_ge(o_done, n * 8 - 2)
                unit(3, d.w_q[0, 1])
                sp.wait_ge(o_done, n * 8)
                unit(4, d.w_q[0, 2])
            sp.wait_ge(acc_add, n * 8 + 8)
            sp.dma_start(d.x2t[b], acc[:, :, :]).then_inc(x2t_out, 16)
            sp.wait_ge(x2t_out, b * 16 + 16)
            if not last:
                sp.dma_start(acc[:, :, :], d.x_t[b + 1]).then_inc(acc_raw, 16)

        sp.dma_start(cx_raw[:, :, :], d.ctx_t[0]).then_inc(ctx_raw, 16)
        first_group(0)
        sp.dma_start(x_rows[:, :, :], d.x_rows[0]).then_inc(rows_raw, 16)
        sp.dma_start(acc[:, :, :], d.x_t[0]).then_inc(acc_raw, 16)
        with sp.Fori(0, BLOCKS - 1) as b:
            do_block(b, last=False)
        do_block(BLOCKS - 1, last=True)

    @block.tensor
    def _(pe):
        def w_ready(b, g, c):
            pe.wait_ge(unit_lo, b * UPB + g * UPG + (c + 1))
            return ring[c % RING]

        def keys_values(n, half, units, ctx_before=None):
            for t in (2 * half, 2 * half + 1):
                tok = slice(t * S, t * S + S)
                out = proj[half][:, (t % 2) * 256:(t % 2) * 256 + 256]
                for kt in range(KT):
                    if ctx_before is not None and t == 0:
                        pe.wait_ge(ctx_lo, ctx_before + (kt + 1))
                    w_hi, w_lo, _ = units[kt // 4]
                    cols = slice((kt % 4) * 256, (kt % 4) * 256 + 256)
                    done = split_product(nc, out, [(cx_hi[:, kt, tok], cx_lo[:, kt, tok], w_hi[:, cols], w_lo[:, cols])],
                                         kt == 0, kt == KT - 1)
            done.then_inc(kv_done, 1)

        def query(j, w):
            for kt in range(KT):
                cols = slice(kt * P, kt * P + P)
                done = split_product(nc, proj[j % 2][:, :], [(w[0][:, cols], w[1][:, cols], xn_hi[:, kt, :], xn_lo[:, kt, :])],
                                     kt == 0, kt == KT - 1)
            done.then_inc(q_done, 1)

        def query_rows(n, j):
            pe.wait_ge(q_copied, n * 4 + (j + 1))
            if j:
                pe.wait_ge(q_squared, n * 4 + j)
            for t in range(TB):
                done = nc.tensor.transpose(bank_t[:, t * S:t * S + S], qt[j % 2][:, t, :], ident[:, :])
            done.then_inc(t1_done, 1)

        def key_columns(n):
            pe.wait_ge(k_scaled, n + 1)
            for t in range(TB):
                done = nc.tensor.transpose(bank_x[:, t * S:t * S + S], k_n[:, t, :], ident[:, :])
            done.then_inc(kt_done, 1)

        def scores(n, j):
            if j == 0:
                pe.wait_ge(kt_copied, n + 1)
            else:
                pe.wait_ge(s_masked, n * 4 + j)
            for t in range(TB):
                done = nc.tensor.matmul(bank_s[:, t * S:t * S + S], qt[j % 2][:, t, :], kt_sb[:, t, :], start=True, stop=True)
            done.then_inc(s_done, 1)

        def probs_columns(n, j):
            pe.wait_ge(p_norm, n * 4 + (j + 1))
            if j:
                pe.wait_ge(pt_lo_done, n * 4 + j)
            for t in range(TB):
                done = nc.tensor.transpose(bank_x[:, t * S:t * S + S], pr[:, t, :], ident[:, :])
            done.then_inc(pt_done, 1)

        def weighted_values(n):
            pe.wait_ge(pt_lo_done, n * 4 + 4)
            for t, bank in enumerate((bank_v, bank_t, bank_o0, bank_o1)):
                if t == 0:
                    pe.wait_ge(v_moved, n + 1)
                if t == 2:
                    pe.wait_ge(acc_add, n * 8 + 8)
                done = split_product(nc, bank[:, :], [(
                    vc_hi[:, t, :], vc_lo[:, t, :],
                    pt_hi[:, t, :, :].rearrange("p h q -> p (h q)"), pt_lo[:, t, :, :].rearrange("p h q -> p (h q)"))],
                    True, True)
                done.then_inc(pv_done, 1)

        def output(n, c, w):
            bank = (bank_o0, bank_o1)[c % 2]
            if c < 2:
                pe.wait_ge(ot_lo_done, n * 4 + 4)
            else:
                pe.wait_ge(acc_add, n * 8 + (c + 7))
            pairs = []
            for h in range(GH):
                cols = slice((c % 2) * 512 + h * P, (c % 2) * 512 + h * P + P)
                pairs.append((w[0][:, cols], w[1][:, cols],
                              ot_hi[:, h, :, :].rearrange("p t q -> p (t q)"), ot_lo[:, h, :, :].rearrange("p t q -> p (t q)")))
            split_product(nc, bank[:, :], pairs, True, True).then_inc(o_done, 1)

        def group(b, g, first):
            n = b * GROUPS + g
            c = 0 if first else FIRST_UNITS - UPG
            units = (w_ready(b, g, c), w_ready(b, g, c + 1))
            keys_values(n, 0, units, b * KT if first else None)
            if not first:
                probs_columns(n - 1, 3)
            keys_values(n, 1, units)
            if first:
                rows_transposed(b)
            else:
                weighted_values(n - 1)
            pe.wait_ge(v_lo_done, n * 2 + 1)
            for j in range(GH):
                k = c + 2 + (j if first else 2 * j)
                if j == 1:
                    pe.wait_ge(v_lo_done, n * 2 + 2)
                query(j, w_ready(b, g, k))
                if not first:
                    w = w_ready(b, g, k + 1)
                    output(n - 1, 2 * j, w)
                query_rows(n, j)
                if j == 0:
                    key_columns(n)
                if not first and j < 3:
                    output(n - 1, 2 * j + 1, w)
                if j:
                    probs_columns(n, j - 1)
                scores(n, j)
            if not first:
                output(n - 1, 7, w)

        def rows_transposed(b):
            pe.wait_ge(row_norm, b * TB + TB)
            pe.wait_ge(acc_add, b * (8 * GROUPS) + 8)
            banks = (bank_o0, bank_o1, bank_t, bank_v)
            for kt in range(KT):
                if kt >= 4:
                    pe.wait_ge(xn_lo_done, b * KT + (kt - 3))
                for t in range(TB):
                    done = nc.tensor.transpose(banks[kt % 4][:, t * S:t * S + S], x_rows[:, t, kt * P:kt * P + P], ident[:, :])
                done.then_inc(xt_done, 1)
            pe.wait_ge(xn_lo_done, b * KT + KT)

        pe.wait_ge(const_in, 16 * CONSTS)
        with pe.Fori(0, BLOCKS) as b:
            group(b, 0, first=True)
            with pe.Fori(1, GROUPS) as g:
                group(b, g, first=False)
            n = b * GROUPS + (GROUPS - 1)
            probs_columns(n, 3)
            weighted_values(n)
            for c in range(8):
                if c % 2 == 0:
                    w = w_ready(b, GROUPS, c // 2 - 4)
                output(n, c, w)

    @block.scalar
    def _(act):
        def split(b, g, c):
            act.wait_ge(unit_raw[c % RING], b * (16 * UPB // RING) + g * (16 * UPG // RING) + 16 * (c // RING + 1))
            nc.scalar.copy(ring[c % RING][0][:, :], ring[c % RING][2][:, :]).then_inc(unit_hi, 1)

        def values_half(n, half):
            act.wait_ge(kv_done, n * 2 + (half + 1))
            bank = proj[half][:, :].rearrange("p (t c) -> p t c", c=256)
            for i in range(2):
                last = nc.scalar.activation(k_sq[:, 2 * half + i, :], bank[:, i, 0:128], ACT.Square,
                                            accum_out=k_ss[:, 2 * half + i:2 * half + i + 1])
            last.then_inc(k_squared, 1)
            nc.scalar.copy(vn_hi[:, 2 * half:2 * half + 2, :], bank[:, :, 128:256]).then_inc(v_hi_done, 1)

        def probs_high(n, j):
            act.wait_ge(pt_done, n * 4 + (j + 1))
            nc.scalar.copy(pt_hi[:, :, j, :], bank_x[:, :].rearrange("p (t q) -> p t q", q=S)).then_inc(pt_hi_done, 1)

        def heads_high(n):
            for t, bank in enumerate((bank_v, bank_t, bank_o0, bank_o1)):
                act.wait_ge(pv_done, n * 4 + (t + 1))
                nc.scalar.copy(ot_hi[:, :, t, :], bank[:, :].rearrange("p (h q) -> p h q", q=S)).then_inc(ot_hi_done, 1)

        def query_copied(n, j):
            act.wait_ge(q_done, n * 4 + (j + 1))
            nc.scalar.copy(qt[j % 2][:, :, :], proj[j % 2][:, :].rearrange("p (t q) -> p t q", q=S)).then_inc(q_copied, 1)

        def query_squares(b, g, n, j):
            act.wait_ge(t1_done, n * 4 + (j + 1))
            for t in range(TB):
                last = nc.scalar.activation(bank_t[:, t * S:t * S + S], bank_t[:, t * S:t * S + S], ACT.Square, accum_out=q_ss[:, t:t + 1])
            last.then_inc(q_squared, 1)
            act.wait_ge(q_squared, n * 4 + (j + 1))
            nc.scalar.activation(q_ln[:, :], q_ss[:, :], ACT.Ln, bias=eps[:, :], scale=1.0 / HEAD_DIM).then_inc(act_step, 1)
            act.wait_ge(act_step, seeds_after(b, g, 1 + j))
            nc.scalar.activation(q_seed[:, :], q_ln[:, :], ACT.Exp, scale=-0.5).then_inc(q_seeded, 1)

        def seeds_after(b, g, item):
            return b * (1 + 5 * GROUPS) + g * 5 + (item + 2)

        def exps(n, j):
            act.wait_ge(s_max, n * 4 + (j + 1))
            for t in range(TB):
                last = nc.scalar.activation(pr[:, t, :], sm[:, t, :], ACT.Exp, bias=nmax[:, t:t + 1], accum_out=rsum[:, t:t + 1])
            last.then_inc(p_exp, 1)

        def group(b, g, first):
            n = b * GROUPS + g
            where = SPLIT_FIRST if first else SPLIT_LATER

            def split_at(place):
                if place in where:
                    split(b, g, where[place])

            split_at(0)
            values_half(n, 0)
            if not first:
                probs_high(n - 1, 3)
            split_at(1)
            values_half(n, 1)
            act.wait_ge(k_squared, n * 2 + 2)
            nc.scalar.activation(k_ln[:, :], k_ss[:, :], ACT.Ln, bias=eps[:, :], scale=1.0 / HEAD_DIM).then_inc(act_step, 1)
            act.wait_ge(act_step, seeds_after(b, g, 0))
            nc.scalar.activation(k_seed[:, :], k_ln[:, :], ACT.Exp, scale=-0.5).then_inc(k_seeded, 1)
            if first:
                banks = (bank_o0, bank_o1, bank_t, bank_v)
                for kt in range(KT):
                    act.wait_ge(xt_done, b * KT + (kt + 1))
                    nc.scalar.copy(xn_hi[:, kt, :], banks[kt % 4][:, :]).then_inc(xn_hi_done, 1)
            else:
                heads_high(n - 1)
            query_copied(n, 0)
            split_at(2)
            query_squares(b, g, n, 0)
            act.wait_ge(kt_done, n + 1)
            nc.scalar.activation(kt_sb[:, :, :], bank_x[:, :].rearrange("p (t q) -> p t q", q=S), ACT.Copy,
                                 scale=kw[:, :]).then_inc(kt_copied, 1)
            split_at(3)
            exps(n, 0)
            for j in (1, 2, 3):
                query_copied(n, j)
                split_at(2 * j + 2)
                query_squares(b, g, n, j)
                probs_high(n, j - 1)
                split_at(2 * j + 3)
                exps(n, j)

        act.wait_ge(const_in, 16 * CONSTS)
        nc.scalar.activation(tgx[:, :], gx[:, :], ACT.Tanh).then_inc(gate_tanh, 1)
        act.preload_act_table_set("natural_log_exp_and_others")
        with act.Fori(0, BLOCKS) as b:
            split(b, 0, 0)
            split(b, 0, 1)
            act.wait_ge(ctx_raw, b * 16 + 16)
            for kt in range(KT):
                nc.scalar.copy(cx_hi[:, kt, :], cx_raw[:, kt, :]).then_inc(ctx_hi, 1)
            split(b, 0, 2)
            act.wait_ge(row_aggr, b * TB + TB)
            nc.scalar.activation(x_ln[:, :], mv[:, :, 1], ACT.Ln, bias=eps[:, :]).then_inc(act_step, 1)
            act.wait_ge(act_step, seeds_after(b, 0, -1))
            nc.scalar.activation(x_seed[:, :], x_ln[:, :], ACT.Exp, scale=-0.5).then_inc(row_seed, 1)
            group(b, 0, first=True)
            with act.Fori(1, GROUPS) as g:
                group(b, g, first=False)
            n = b * GROUPS + (GROUPS - 1)
            probs_high(n, 3)
            split(b, GROUPS, -1)
            heads_high(n)

    @block.vector
    def _(dve):
        def split(b, g, c):
            hi, lo, raw = ring[c % RING]
            dve.wait_ge(unit_hi, b * UPB + g * UPG + (c + 1))
            nc.vector.tensor_tensor(lo[:, :], raw[:, :], hi[:, :].bitcast(FP32), ALU.subtract).then_inc(unit_lo, 1)

        def low(out, whole, hi):
            return nc.vector.tensor_tensor(out, whole, hi.bitcast(FP32), ALU.subtract)

        def alone():
            dve.sem_inc(vector_waited, 1)

        def values_half(n, half):
            bank = proj[half][:, :].rearrange("p (t c) -> p t c", c=256)
            dve.wait_ge(v_hi_done, n * 2 + (half + 1))
            nc.vector.tensor_copy(k_sb[:, 2 * half:2 * half + 2, :], bank[:, :, 0:128]).then_inc(k_copied, 1)
            low(vn_lo[:, 2 * half:2 * half + 2, :], bank[:, :, 128:256],
                vn_hi[:, 2 * half:2 * half + 2, :]).then_inc(v_lo_done, 1)

        def probs_low(n, j):
            dve.wait_ge(pt_hi_done, n * 4 + (j + 1))
            low(pt_lo[:, :, j, :], bank_x[:, :].rearrange("p (t q) -> p t q", q=S), pt_hi[:, :, j, :]).then_inc(pt_lo_done, 1)

        def heads_low(n):
            for t, bank in enumerate((bank_v, bank_t, bank_o0, bank_o1)):
                dve.wait_ge(ot_hi_done, n * 4 + (t + 1))
                low(ot_lo[:, :, t, :], bank[:, :].rearrange("p (h q) -> p h q", q=S), ot_hi[:, :, t, :]).then_inc(ot_lo_done, 1)

        def add_output(b, n, c):
            dve.wait_ge(o_done, n * 8 + (c + 1))
            nc.vector.scalar_tensor_tensor(acc[:, c, :], (bank_o0, bank_o1)[c % 2][:, :], tgx[:, :], acc[:, c, :],
                                           ALU.mult, ALU.add).then_inc(acc_add, 1)

        def softmax_max(b, g, n, j):
            dve.wait_ge(s_done, n * 4 + (j + 1))
            dve.wait_ge(rstd_step, newton_after(b, g, QUERIES + j))
            for t in range(TB):
                last = nc.vector.scalar_tensor_tensor(sm[:, t, :], bank_s[:, t * S:t * S + S], q_rstd[:, t:t + 1], mask[:, :],
                                                      ALU.mult, ALU.add)
            last.then_inc(s_masked, 1)
            dve.wait_ge(s_masked, n * 4 + (j + 1))
            nc.vector.tensor_reduce(nmax[:, :], sm[:, :, :], AX.X, ALU.max, negate=True).then_inc(s_max, 1)

        def softmax_norm(n, j):
            dve.wait_ge(p_exp, n * 4 + (j + 1))
            nc.vector.reciprocal(rinv[:, :], rsum[:, :]).then_inc(p_inv, 1)
            dve.wait_ge(p_inv, n * 4 + (j + 1))
            nc.vector.tensor_tensor(pr[:, :, :], pr[:, :, :], rinv[:, :].unsqueeze(2).to_broadcast([P, TB, S]),
                                    ALU.mult).then_inc(p_norm, 1)

        def normalise_rows(b):
            dve.wait_ge(rstd_step, newton_after(b, 0, ROWS))
            for t in range(TB):
                nc.vector.tensor_scalar(x_rows[:, t, :], x_rows[:, t, :], mv[:, t, 0:1], x_rstd[:, t:t + 1],
                                        ALU.subtract, ALU.mult).then_inc(row_norm, 1)

        def group(b, g, first):
            n = b * GROUPS + g
            where = SPLIT_FIRST if first else SPLIT_LATER

            def split_at(place):
                if place in where:
                    split(b, g, where[place])

            split_at(0)
            if first:
                normalise_rows(b)
            values_half(n, 0)
            if not first:
                probs_low(n - 1, 3)
            split_at(1)
            values_half(n, 1)
            if first:
                banks = (bank_o0, bank_o1, bank_t, bank_v)
                for kt in range(KT):
                    dve.wait_ge(xn_hi_done, b * KT + (kt + 1))
                    low(xn_lo[:, kt, :], banks[kt % 4][:, :], xn_hi[:, kt, :]).then_inc(xn_lo_done, 1)
            else:
                heads_low(n - 1)
            split_at(2)
            if not first:
                add_output(b, n - 1, 0)
                add_output(b, n - 1, 1)
            softmax_max(b, g, n, 0)
            split_at(3)
            softmax_norm(n, 0)
            for j in (1, 2, 3):
                if not first:
                    add_output(b, n - 1, 2 * j)
                    if j < 3:
                        add_output(b, n - 1, 2 * j + 1)
                split_at(2 * j + 2)
                probs_low(n, j - 1)
                softmax_max(b, g, n, j)
                split_at(2 * j + 3)
                softmax_norm(n, j)
            if not first:
                add_output(b, n - 1, 7)

        dve.wait_ge(const_in, 16 * CONSTS)
        nc.vector.tensor_scalar(kw[:, :], nw[:, 0:1], nw[:, 1:2], float(HEAD_DIM) ** -0.5, ALU.mult, ALU.mult).then_inc(kw_set, 1)
        dve.wait_ge(kw_set, 1)
        dve.wait_ge(gate_tanh, 1)
        nc.vector.tensor_copy(rinv[:, 0:1], tgx[:, :]).then_inc(acc_add, 8)
        with dve.Fori(0, BLOCKS) as b:
            split(b, 0, 0)
            split(b, 0, 1)
            for kt in range(KT):
                dve.wait_ge(ctx_hi, b * KT + (kt + 1))
                low(cx_lo[:, kt, :], cx_raw[:, kt, :], cx_hi[:, kt, :]).then_inc(ctx_lo, 1)
            split(b, 0, 2)
            dve.wait_ge(rows_raw, b * 16 + 16)
            for t in range(TB):
                for i in range(2):
                    last = nc.vector.bn_stats(stats[:, t, i, :], x_rows[:, t, i * 512:i * 512 + 512])
            last.then_inc(row_stats, 1)
            dve.wait_ge(row_stats, b + 1)
            alone()
            for t in range(TB):
                nc.vector.bn_aggr(mv[:, t, :], stats[:, t, :, :].rearrange("p i s -> p (i s)")).then_inc(row_aggr, 1)
            group(b, 0, first=True)
            dve.wait_ge(acc_raw, b * 16 + 16)
            alone()
            with dve.Fori(1, GROUPS) as g:
                group(b, g, first=False)
            n = b * GROUPS + (GROUPS - 1)
            probs_low(n, 3)
            split(b, GROUPS, -1)
            heads_low(n)
            for c in range(8):
                add_output(b, n, c)

    @block.gpsimd
    def _(pool):
        def alone():
            pool.sem_inc(pool_waited, 1)

        def newton(ss, scale, seed, v, t, out, after):
            nc.gpsimd.tensor_scalar(v[:, :], ss, scale, EPS, ALU.mult, ALU.add).then_inc(rstd_step, 1)
            nc.gpsimd.tensor_tensor(t[:, :], seed[:, :], seed[:, :], ALU.mult).then_inc(rstd_step, 1)
            pool.wait_ge(rstd_step, after - 3)
            nc.gpsimd.tensor_tensor(t[:, :], t[:, :], v[:, :], ALU.mult).then_inc(rstd_step, 1)
            pool.wait_ge(rstd_step, after - 2)
            alone()
            nc.gpsimd.tensor_scalar(t[:, :], t[:, :], -0.5, 1.5, ALU.mult, ALU.add).then_inc(rstd_step, 1)
            pool.wait_ge(rstd_step, after - 1)
            nc.gpsimd.tensor_tensor(out[:, :], t[:, :], seed[:, :], ALU.mult).then_inc(rstd_step, 1)

        def group(b, g):
            n = b * GROUPS + g
            pool.wait_ge(k_seeded, n + 1)
            alone()
            after = newton_after(b, g, KEYS)
            newton(k_ss[:, :], 1.0 / HEAD_DIM, k_seed, k_v, k_t, k_rstd, after)
            pool.wait_ge(rstd_step, after)
            pool.wait_ge(k_copied, n * 2 + 2)
            nc.gpsimd.tensor_tensor(k_n[:, :, :], k_sb[:, :, :], k_rstd[:, :].unsqueeze(2).to_broadcast([P, TB, HEAD_DIM]),
                                    ALU.mult).then_inc(k_scaled, 1)
            for j in range(GH):
                pool.wait_ge(q_seeded, n * 4 + (j + 1))
                alone()
                newton(q_ss[:, :], 1.0 / HEAD_DIM, q_seed, q_v, q_t, q_rstd, newton_after(b, g, QUERIES + j))
                if j == 0:
                    pool.wait_ge(v_lo_done, n * 2 + 2)
                    alone()
                    nc.gpsimd.tensor_copy(vc_hi[:, :, :], vn_hi[:, :, :].bitcast(FP32))
                    nc.gpsimd.tensor_copy(vc_lo[:, :, :], vn_lo[:, :, :].bitcast(FP32)).then_inc(v_moved, 1)

        with pool.Fori(0, BLOCKS) as b:
            pool.wait_ge(row_seed, b + 1)
            alone()
            newton(mv[:, :, 1], 1.0, x_seed, x_v, x_t, x_rstd, newton_after(b, 0, ROWS))
            group(b, 0)
            with pool.Fori(1, GROUPS) as g:
                group(b, g)


def ffn_phase(nc, ctx, sem, psum, d):
    a = Arena(nc, "ff")
    ring = [a.pair(f"ring{s}", [P, UNIT], raw=True) for s in range(FFN_RING)]
    wr_hi, wr_lo, wr_raw = a.pair("router", [P, KT, P], raw=True)
    x2_ln = a.put("x2_ln", [P, KT, TOK])
    x2_res = a.put("x2_res", [P, KT, TOK])
    rows = a.put("rows", [P, TB, HIDDEN])
    xn_hi, xn_lo = a.pair("xn", [P, KT, TOK])
    hg_hi, hg_lo = a.pair("hg", [P, KT, TOK])
    expand_in = a.put("expand_in", [P, KT, P])
    expand = a.put("expand", [P, KT, P], FP32R)
    gt_hi, gt_lo = a.pair("gt", [P, TOK])
    sct = a.put("router_scores_t", [P, TB, S])
    sc, w1, w2, sel, ex = (a.put(k, [P, TB, EXPERTS]) for k in ("scores", "without8", "without16", "chosen", "exps"))
    gates = a.put("gates", [P, TB, P])
    m1, m2 = a.put("top8", [P, TB, 8]), a.put("next8", [P, TB, 8])
    g_nmax, g_sum, g_inv = a.put("g_neg_max", [P, TB]), a.put("g_sum", [P, TB]), a.put("g_inv", [P, TB])
    g_rep = [a.put(f"gates_of_ranks{i}", [P, TOK]) for i in range(2)]
    hg = [a.put(f"hg{i}", [P, TOK]) for i in range(2)]
    ident = a.put("ident", [P, P])
    eps, g_in, tg, tg2 = (a.put(k, [P, 1]) for k in ("eps", "gate_in", "gate", "gate_scaled"))
    stats, mv = a.put("stats", [P, TB, 2, 6]), a.put("mean_var", [P, TB, 2])
    ln, seed, nv, nt, rstd = (a.put("row_" + k, [P, TB]) for k in ("ln", "seed", "v", "t", "rstd"))
    assert a.at <= nc.sbuf_top, a.at

    bank_h, bank_e, bank_x = psum[0:4], psum[4:6], psum[6:8]
    prep_banks = (bank_x[0], bank_x[1], bank_e[0], bank_e[1])

    const_in, x2_ln_in, x2_res_in, y_out = sem("f_const_in"), sem("x2_ln_in"), sem("x2_res_in"), sem("y_out")
    unit_raw = [sem(f"f_unit_raw{s}") for s in range(FFN_RING)]
    gate_tanh, gate_set, gates_zero = sem("f_gate_tanh"), sem("f_gate_set"), sem("gates_zero")
    unit_hi, unit_lo, router_hi, router_lo = sem("f_unit_hi"), sem("f_unit_lo"), sem("router_hi"), sem("router_lo")
    tt_done, row_stats, row_aggr, row_ln, row_seed, row_norm, rstd_step = (
        sem(k) for k in ("tt_done", "f_row_stats", "f_row_aggr", "row_ln", "f_row_seed", "f_row_norm", "f_rstd_step"))
    xt_done, xn_hi_done, xn_lo_done = sem("f_xt_done"), sem("f_xn_hi_done"), sem("f_xn_lo_done")
    r_done, sct_copied, st_done, gate_step, gate_max, gate_exp, gates_done = (
        sem(k) for k in ("r_done", "sct_copied", "st_done", "gate_step", "gate_max", "gate_exp", "gates_done"))
    gt_done, gt_hi_done, gt_lo_done = sem("gt_done"), sem("gt_hi_done"), sem("gt_lo_done")
    h_done, e_done, g_copied, hg_done, hg_hi_done, hg_lo_done = (
        sem(k) for k in ("h_done", "e_done", "g_copied", "hg_done", "hg_hi_done", "hg_lo_done"))
    y_done, y_add = sem("y_done"), sem("y_add")
    vector_waited, pool_waited = sem("f_vector_waited"), sem("f_pool_waited")

    CONSTS = 5
    UNITS = 2 * KT
    GATE_STEPS = 8
    block = ctx.enter_context(nc.Block())

    @block.sync
    def _(sp):
        def unit(k, src):
            sp.dma_start(ring[k % FFN_RING][2][:, :], src).then_inc(unit_raw[k % FFN_RING], 16)

        def do_block(b, last):
            for c in range(FFN_RING, KT):
                sp.wait_ge(h_done, b * KT + (c - 3))
                unit(c, d.w_a[c])
            if not last:
                sp.wait_ge(tt_done, b * TB + TB)
                sp.dma_start(x2_ln[:, :, :], d.x2t[b + 1]).then_inc(x2_ln_in, 16)
            for c in range(FFN_RING):
                sp.wait_ge(h_done, b * KT + (c + 5))
                unit(c, d.w_b[c])
            for c in range(KT):
                sp.wait_ge(y_done, b * KT + (c + 1))
                if c < FFN_RING:
                    unit(c, d.w_b[c + FFN_RING])
                elif not last:
                    unit(c, d.w_a[c - FFN_RING])
                sp.wait_ge(y_add, b * KT + (KT + c + 1))
                sp.dma_start(d.y_t[b, :, c, :], x2_res[:, c, :]).then_inc(y_out, 16)
            sp.wait_ge(y_out, b * (16 * KT) + 16 * KT)
            if not last:
                sp.dma_start(x2_res[:, :, :], d.x2t[b + 1]).then_inc(x2_res_in, 16)

        sp.dma_start(x2_ln[:, :, :], d.x2t[0]).then_inc(x2_ln_in, 16)
        sp.dma_start(g_in[:, :], d.g_f).then_inc(const_in, 16)
        sp.dma_start(ident[:, :], d.ident).then_inc(const_in, 16)
        sp.dma_start(eps[:, :], d.eps).then_inc(const_in, 16)
        sp.dma_start(expand_in[:, :, :], d.expand).then_inc(const_in, 16)
        sp.dma_start(wr_raw[:, :, :], d.w_r.rearrange("p (k o) -> p k o", k=KT)).then_inc(const_in, 16)
        for c in range(FFN_RING):
            unit(c, d.w_a[c])
        sp.dma_start(x2_res[:, :, :], d.x2t[0]).then_inc(x2_res_in, 16)
        with sp.Fori(0, BLOCKS - 1) as b:
            do_block(b, last=False)
        do_block(BLOCKS - 1, last=True)

    @block.tensor
    def _(pe):
        def token_rows(b, t):
            if t == 0:
                pe.wait_ge(x2_ln_in, b * 16 + 16)
            if t >= 2:
                pe.wait_ge(row_norm, b * TB + (t - 1))
            for kt in range(KT):
                bank = prep_banks[2 * (t % 2) + kt // 4]
                done = nc.tensor.transpose(bank[:, (kt % 4) * P:(kt % 4) * P + P], x2_ln[:, kt, t * S:t * S + S], ident[:, :])
            done.then_inc(tt_done, 1)

        def hidden_columns(b, kts):
            for kt in kts:
                if kt == 0:
                    pe.wait_ge(row_norm, b * TB + TB)
                if kt >= 4:
                    pe.wait_ge(xn_lo_done, b * KT + (kt - 3))
                for t in range(TB):
                    done = nc.tensor.transpose(prep_banks[kt % 4][:, t * S:t * S + S], rows[:, t, kt * P:kt * P + P], ident[:, :])
                done.then_inc(xt_done, 1)

        def times_xn(bank, w, done_sem, b=None):
            for kt in range(KT):
                if b is not None:
                    pe.wait_ge(xn_lo_done, b * KT + (kt + 1))
                done = split_product(nc, bank[:, :], [(w[0][:, kt, :], w[1][:, kt, :], xn_hi[:, kt, :], xn_lo[:, kt, :])],
                                     kt == 0, kt == KT - 1)
            done.then_inc(done_sem, 1)

        def w_ready(b, k):
            pe.wait_ge(unit_lo, b * UNITS + (k + 1))
            return [w[:, :].rearrange("p (k o) -> p k o", k=KT) for w in ring[k % FFN_RING][:2]]

        def ranks(b, c):
            w = w_ready(b, c)
            if c < 2:
                pe.wait_ge(y_add, b * KT + (KT - 1 + c))
            if c >= 4:
                pe.wait_ge(hg_done, b * KT + (c - 3))
            times_xn(bank_h[c % 4], w, h_done)

        def gates_of_ranks(b, c):
            if c == 0:
                pe.wait_ge(gt_lo_done, b + 1)
            if c >= 2:
                pe.wait_ge(g_copied, b * KT + (c - 1))
            nc.tensor.matmul(bank_e[c % 2][:, :], expand[:, c, :], gt_hi[:, :], start=True, stop=False)
            nc.tensor.matmul(bank_e[c % 2][:, :], expand[:, c, :], gt_lo[:, :], start=False, stop=True).then_inc(e_done, 1)

        def output(b, o):
            w = w_ready(b, KT + o)
            if o >= 2:
                pe.wait_ge(y_add, b * KT + (KT + o - 1))
            else:
                pe.wait_ge(hg_done, b * KT + (5 + o))
            for c in range(KT):
                if o == 0:
                    pe.wait_ge(hg_lo_done, b * KT + (c + 1))
                done = split_product(nc, bank_h[o % 2][:, :], [(w[0][:, c, :], w[1][:, c, :], hg_hi[:, c, :], hg_lo[:, c, :])],
                                     c == 0, c == KT - 1)
            done.then_inc(y_done, 1)

        def do_block(b, last):
            times_xn(bank_h[3], (wr_hi, wr_lo), r_done, b)
            ranks(b, 0)
            pe.wait_ge(sct_copied, b + 1)
            for t in range(TB):
                done = nc.tensor.transpose(bank_x[0][:, t * P:t * P + P], sct[:, t, :], ident[:, :])
            done.then_inc(st_done, 1)
            ranks(b, 1)
            ranks(b, 2)
            pe.wait_ge(gates_done, b + 1)
            for t in range(TB):
                done = nc.tensor.transpose(bank_x[1][:, t * S:t * S + S], gates[:, t, :], ident[:, :])
            done.then_inc(gt_done, 1)
            ranks(b, 3)
            gates_of_ranks(b, 0)
            gates_of_ranks(b, 1)
            for c in range(4, KT):
                ranks(b, c)
                gates_of_ranks(b, c - 2)
            gates_of_ranks(b, 6)
            gates_of_ranks(b, 7)
            output(b, 0)
            if last:
                for o in range(1, KT):
                    output(b, o)
                return
            token_rows(b + 1, 0)
            token_rows(b + 1, 1)
            output(b, 1)
            token_rows(b + 1, 2)
            output(b, 2)
            token_rows(b + 1, 3)
            output(b, 3)
            hidden_columns(b + 1, range(0, 4))
            output(b, 4)
            hidden_columns(b + 1, range(4, 8))
            for o in range(5, KT):
                output(b, o)

        pe.wait_ge(const_in, 16 * CONSTS)
        for t in range(TB):
            token_rows(0, t)
        hidden_columns(0, range(KT))
        pe.wait_ge(router_lo, 1)
        with pe.Fori(0, BLOCKS - 1) as b:
            do_block(b, last=False)
        do_block(BLOCKS - 1, last=True)

    @block.scalar
    def _(act):
        def split(b, k):
            act.wait_ge(unit_raw[k % FFN_RING], b * (16 * UNITS // FFN_RING) + 16 * (k // FFN_RING + 1))
            nc.scalar.copy(ring[k % FFN_RING][0][:, :], ring[k % FFN_RING][2][:, :]).then_inc(unit_hi, 1)

        def row_seeds(b, t):
            act.wait_ge(row_aggr, b * TB + (t + 1))
            nc.scalar.activation(ln[:, t:t + 1], mv[:, t, 1:2], ACT.Ln, bias=eps[:, :]).then_inc(row_ln, 1)
            act.wait_ge(row_ln, b * TB + (t + 1))
            nc.scalar.activation(seed[:, t:t + 1], ln[:, t:t + 1], ACT.Exp, scale=-0.5).then_inc(row_seed, 1)

        def columns_high(b, kts):
            for kt in kts:
                act.wait_ge(xt_done, b * KT + (kt + 1))
                nc.scalar.copy(xn_hi[:, kt, :], prep_banks[kt % 4][:, :]).then_inc(xn_hi_done, 1)

        def gates_copied(b, c):
            act.wait_ge(e_done, b * KT + (c + 1))
            nc.scalar.copy(g_rep[c % 2][:, :], bank_e[c % 2][:, :]).then_inc(g_copied, 1)

        def gated_high(b, c):
            act.wait_ge(hg_done, b * KT + (c + 1))
            nc.scalar.copy(hg_hi[:, c, :], hg[c % 2][:, :]).then_inc(hg_hi_done, 1)

        def do_block(b, last):
            act.wait_ge(r_done, b + 1)
            nc.scalar.copy(sct[:, :, :], bank_h[3][:, :].rearrange("p (t q) -> p t q", q=S)).then_inc(sct_copied, 1)
            split(b, 2)
            split(b, 3)
            act.wait_ge(gate_max, b + 1)
            for t in range(TB):
                done = nc.scalar.activation(ex[:, t, :], sc[:, t, :], ACT.Exp, bias=g_nmax[:, t:t + 1])
            done.then_inc(gate_exp, 1)
            act.wait_ge(gt_done, b + 1)
            nc.scalar.copy(gt_hi[:, :], bank_x[1][:, :]).then_inc(gt_hi_done, 1)
            split(b, 4)
            gates_copied(b, 0)
            for c in range(1, KT):
                gates_copied(b, c)
                gated_high(b, c - 1)
                if c < 5:
                    split(b, c + 4)
            split(b, 9)
            gated_high(b, 7)
            split(b, 10)
            split(b, 11)
            if last:
                for k in range(12, UNITS):
                    split(b, k)
                return
            row_seeds(b + 1, 0)
            row_seeds(b + 1, 1)
            split(b, 12)
            row_seeds(b + 1, 2)
            split(b, 13)
            row_seeds(b + 1, 3)
            split(b, 14)
            columns_high(b + 1, range(0, 4))
            split(b, 15)
            columns_high(b + 1, range(4, 8))
            split(b, 16)
            split(b, 17)

        act.wait_ge(const_in, 16 * CONSTS)
        nc.scalar.activation(tg[:, :], g_in[:, :], ACT.Tanh).then_inc(gate_tanh, 1)
        act.preload_act_table_set("natural_log_exp_and_others")
        for t in range(TB):
            row_seeds(0, t)
        nc.scalar.copy(wr_hi[:, :, :], wr_raw[:, :, :]).then_inc(router_hi, 1)
        nc.scalar.copy(expand[:, :, :], expand_in[:, :, :]).then_inc(router_hi, 1)
        split(0, 0)
        columns_high(0, range(KT))
        split(0, 1)
        with act.Fori(0, BLOCKS - 1) as b:
            do_block(b, last=False)
        do_block(BLOCKS - 1, last=True)

    @block.vector
    def _(dve):
        def low(out, whole, hi):
            return nc.vector.tensor_tensor(out, whole, hi.bitcast(FP32), ALU.subtract)

        def alone():
            dve.sem_inc(vector_waited, 1)

        def split(b, k):
            hi, lo, raw = ring[k % FFN_RING]
            dve.wait_ge(unit_hi, b * UNITS + (k + 1))
            low(lo[:, :], raw[:, :], hi[:, :]).then_inc(unit_lo, 1)

        def row_statistics(b, t):
            dve.wait_ge(tt_done, b * TB + (t + 1))
            for i in range(2):
                done = nc.vector.bn_stats(stats[:, t, i, :], prep_banks[2 * (t % 2) + i][:, :])
            done.then_inc(row_stats, 1)
            dve.wait_ge(row_stats, b * TB + (t + 1))
            alone()
            nc.vector.bn_aggr(mv[:, t, :], stats[:, t, :, :].rearrange("p i s -> p (i s)")).then_inc(row_aggr, 1)

        def normalise_rows(b, t):
            dve.wait_ge(rstd_step, b * (5 * TB) + 5 * (t + 1))
            for i in range(2):
                done = nc.vector.tensor_scalar(rows[:, t, i * 512:i * 512 + 512], prep_banks[2 * (t % 2) + i][:, :],
                                               mv[:, t, 0:1], rstd[:, t:t + 1], ALU.subtract, ALU.mult)
            done.then_inc(row_norm, 1)

        def columns_low(b, kts):
            for kt in kts:
                dve.wait_ge(xn_hi_done, b * KT + (kt + 1))
                low(xn_lo[:, kt, :], prep_banks[kt % 4][:, :], xn_hi[:, kt, :]).then_inc(xn_lo_done, 1)

        def choose(b):
            dve.wait_ge(st_done, b + 1)
            step = b * GATE_STEPS
            nc.vector.tensor_copy(sc[:, :, :], bank_x[0][:, :].rearrange("p (t e) -> p t e", e=P)[:, :, 0:EXPERTS]).then_inc(gate_step, 1)
            dve.wait_ge(gate_step, step + 1)
            alone()
            for t in range(TB):
                done = nc.vector.max(m1[:, t, :], sc[:, t, :])
            done.then_inc(gate_step, 1)
            dve.wait_ge(gate_step, step + 2)
            alone()
            nc.vector.tensor_scalar(g_nmax[:, :], m1[:, :, 0], -1.0, None, ALU.mult).then_inc(gate_max, 1)
            for t in range(TB):
                done = nc.vector.match_replace(w1[:, t, :], m1[:, t, :], sc[:, t, :], LOWEST)
            done.then_inc(gate_step, 1)
            dve.wait_ge(gate_step, step + 3)
            alone()
            for t in range(TB):
                done = nc.vector.max(m2[:, t, :], w1[:, t, :])
            done.then_inc(gate_step, 1)
            dve.wait_ge(gate_step, step + 4)
            alone()
            for t in range(TB):
                done = nc.vector.match_replace(w2[:, t, :], m2[:, t, :], w1[:, t, :], LOWEST)
            done.then_inc(gate_step, 1)
            dve.wait_ge(gate_step, step + 5)
            nc.vector.tensor_tensor(sel[:, :, :], w2[:, :, :], sc[:, :, :], ALU.not_equal).then_inc(gate_step, 1)

        def gate_softmax(b):
            step = b * GATE_STEPS
            dve.wait_ge(gate_exp, b + 1)
            dve.wait_ge(gate_step, step + 6)
            nc.vector.tensor_tensor(w1[:, :, :], ex[:, :, :], sel[:, :, :], ALU.mult).then_inc(gate_step, 1)
            dve.wait_ge(gate_step, step + 7)
            nc.vector.tensor_reduce(g_sum[:, :], w1[:, :, :], AX.X, ALU.add).then_inc(gate_step, 1)
            dve.wait_ge(gate_step, step + 8)
            nc.vector.reciprocal(g_inv[:, :], g_sum[:, :]).then_inc(gate_set, 1)
            dve.wait_ge(gate_set, b + 2)
            nc.vector.tensor_tensor(gates[:, :, 0:EXPERTS], w1[:, :, :], g_inv[:, :].unsqueeze(2).to_broadcast([P, TB, EXPERTS]),
                                    ALU.mult).then_inc(gates_done, 1)

        def gated(b, c):
            dve.wait_ge(g_copied, b * KT + (c + 1))
            nc.vector.tensor_tensor(hg[c % 2][:, :], bank_h[c % 4][:, :], g_rep[c % 2][:, :], ALU.mult).then_inc(hg_done, 1)
            dve.wait_ge(hg_hi_done, b * KT + (c + 1))
            low(hg_lo[:, c, :], hg[c % 2][:, :], hg_hi[:, c, :]).then_inc(hg_lo_done, 1)

        def add_output(b, o):
            dve.wait_ge(y_done, b * KT + (o + 1))
            if o == 0:
                dve.wait_ge(x2_res_in, b * 16 + 16)
            nc.vector.scalar_tensor_tensor(x2_res[:, o, :], bank_h[o % 2][:, :], tg2[:, :], x2_res[:, o, :],
                                           ALU.mult, ALU.add).then_inc(y_add, 1)

        def do_block(b, last):
            split(b, 2)
            choose(b)
            split(b, 3)
            gate_softmax(b)
            dve.wait_ge(gt_hi_done, b + 1)
            low(gt_lo[:, :], bank_x[1][:, :], gt_hi[:, :]).then_inc(gt_lo_done, 1)
            split(b, 4)
            for c in range(KT - 1):
                gated(b, c)
                if c < 4:
                    split(b, c + 5)
            split(b, 9)
            gated(b, 7)
            split(b, 10)
            split(b, 11)
            add_output(b, 0)
            if last:
                for o in range(1, KT):
                    if o < 5:
                        split(b, 11 + o)
                    add_output(b, o)
                return
            row_statistics(b + 1, 0)
            row_statistics(b + 1, 1)
            normalise_rows(b + 1, 0)
            normalise_rows(b + 1, 1)
            add_output(b, 1)
            split(b, 12)
            row_statistics(b + 1, 2)
            normalise_rows(b + 1, 2)
            add_output(b, 2)
            split(b, 13)
            row_statistics(b + 1, 3)
            normalise_rows(b + 1, 3)
            add_output(b, 3)
            split(b, 14)
            columns_low(b + 1, range(0, 4))
            add_output(b, 4)
            split(b, 15)
            columns_low(b + 1, range(4, 8))
            add_output(b, 5)
            split(b, 16)
            add_output(b, 6)
            split(b, 17)
            add_output(b, 7)

        dve.wait_ge(gate_tanh, 1)
        nc.vector.tensor_scalar(tg2[:, :], tg[:, :], ALPHA_OVER_RANK, None, ALU.mult).then_inc(gate_set, 1)
        dve.wait_ge(gate_set, 1)
        nc.vector.memset(gates[:, :, EXPERTS:], 0.0).then_inc(y_add, KT)
        row_statistics(0, 0)
        row_statistics(0, 1)
        normalise_rows(0, 0)
        normalise_rows(0, 1)
        row_statistics(0, 2)
        row_statistics(0, 3)
        normalise_rows(0, 2)
        normalise_rows(0, 3)
        dve.wait_ge(router_hi, 2)
        low(wr_lo[:, :, :], wr_raw[:, :, :], wr_hi[:, :, :]).then_inc(router_lo, 1)
        split(0, 0)
        columns_low(0, range(KT))
        split(0, 1)
        with dve.Fori(0, BLOCKS - 1) as b:
            do_block(b, last=False)
        do_block(BLOCKS - 1, last=True)

    @block.gpsimd
    def _(pool):
        def alone():
            pool.sem_inc(pool_waited, 1)

        def newton(b, t):
            after = b * (5 * TB) + 5 * (t + 1)
            v, y, z = nv[:, t:t + 1], seed[:, t:t + 1], nt[:, t:t + 1]
            pool.wait_ge(row_seed, b * TB + (t + 1))
            alone()
            nc.gpsimd.tensor_scalar(v, mv[:, t, 1:2], EPS, None, ALU.add).then_inc(rstd_step, 1)
            nc.gpsimd.tensor_tensor(z, y, y, ALU.mult).then_inc(rstd_step, 1)
            pool.wait_ge(rstd_step, after - 3)
            nc.gpsimd.tensor_tensor(z, z, v, ALU.mult).then_inc(rstd_step, 1)
            pool.wait_ge(rstd_step, after - 2)
            alone()
            nc.gpsimd.tensor_scalar(z, z, -0.5, 1.5, ALU.mult, ALU.add).then_inc(rstd_step, 1)
            pool.wait_ge(rstd_step, after - 1)
            nc.gpsimd.tensor_tensor(rstd[:, t:t + 1], z, y, ALU.mult).then_inc(rstd_step, 1)

        with pool.Fori(0, BLOCKS) as b:
            for t in range(TB):
                newton(b, t)


def build(nc, d):
    with ExitStack() as ctx:
        psum = [ctx.enter_context(nc.psum_tensor(f"bank{i}", [P, 512], FP32)) for i in range(8)]
        for phase in (attention_phase, ffn_phase):
            with ExitStack() as part:
                phase(nc, part, lambda name: part.enter_context(nc.semaphore(name)), psum, d)


def lay_out(i):
    import numpy as np

    x, c = i["x"].reshape(BLOCKS, TOK, HIDDEN), i["ctx_4096"].reshape(BLOCKS, TOK, HIDDEN)

    def columns(a):
        return a.transpose(0, 2, 1).reshape(BLOCKS, KT, P, TOK).transpose(0, 2, 1, 3)

    def by_slice(w, outs):
        return w.reshape(-1, outs, KT, P).transpose(0, 3, 2, 1)

    wk, wv = by_slice(i["L0_xattn_k_proj_w"], P), by_slice(i["L0_xattn_v_proj_w"], P)
    kv = np.concatenate([wk, wv], axis=3).reshape(GROUPS, P, 2, UNIT).transpose(0, 2, 1, 3)
    o = i["L0_xattn_o_proj_w"].reshape(KT // 2, 2, P, GROUPS, GH, HEAD_DIM).transpose(3, 0, 5, 1, 4, 2)
    b = i["L0_ffn_B"].transpose(0, 2, 1).reshape(KT, P, KT, P).transpose(2, 1, 0, 3)
    wr = np.concatenate([i["L0_ffn_Wr"], np.zeros((P - EXPERTS, HIDDEN), np.float32)])
    rank_of = np.zeros((P, KT, P), np.float32)
    for j in range(LORA):
        rank_of[j // RANK, j // P, j % P] = 1.0
    out = {
        "x_rows": x.reshape(BLOCKS, TB, P, HIDDEN).transpose(0, 2, 1, 3),
        "x_t": columns(x), "ctx_t": columns(c),
        "w_kv": kv, "w_q": by_slice(i["L0_xattn_q_proj_w"], P).reshape(GROUPS, GH, P, UNIT),
        "w_o": o.reshape(GROUPS, KT // 2, P, UNIT),
        "mask": i["mask_1x1xSxS2_ff0"].reshape(S, S),
        "norm_w": np.stack([i["L0_xattn_q_norm_w"], i["L0_xattn_k_norm_w"]], axis=1),
        "g_x": np.broadcast_to(i["g_xattn"].reshape(1, 1), (P, 1)),
        "g_f": np.broadcast_to(i["g_ffn"].reshape(1, 1), (P, 1)),
        "ident": np.eye(P, dtype=np.float32), "eps": np.full((P, 1), EPS, np.float32),
        "w_a": by_slice(i["L0_ffn_A"].reshape(LORA, HIDDEN), P).reshape(KT, P, UNIT),
        "w_b": b.reshape(KT, P, UNIT), "w_r": by_slice(wr, P).reshape(P, UNIT),
        "expand": rank_of,
    }
    return {k: np.ascontiguousarray(v) for k, v in out.items()}


class Declared:

    def __init__(self, nc, arrays):
        def arg(name):
            return nc.dram_tensor(f"in_{name}", arrays[name].shape, FP32, kind="ExternalInput").ap()

        self.x_rows = arg("x_rows")
        self.x_t = arg("x_t")
        self.ctx_t = arg("ctx_t")
        self.w_kv = arg("w_kv")
        self.w_q = arg("w_q")
        self.w_o = arg("w_o")
        self.mask = arg("mask")
        self.norm_w = arg("norm_w")
        self.g_x = arg("g_x")
        self.g_f = arg("g_f")
        self.ident = arg("ident")
        self.eps = arg("eps")
        self.w_a = arg("w_a")
        self.w_b = arg("w_b")
        self.w_r = arg("w_r")
        self.expand = arg("expand")
        self.x2t = nc.dram_tensor("x2t", (BLOCKS, P, KT, TOK), FP32).ap()
        self.y_t = nc.dram_tensor("out_y", (BLOCKS, P, KT, TOK), FP32, kind="ExternalOutput").ap()


def kernel(**inputs):
    import numpy as np
    from concourse.bacc import Bacc
    from concourse.bass_utils import run_bass_kernel_spmd

    arrays = lay_out({k: np.asarray(v) for k, v in inputs.items()})
    nc = Bacc("TRN2", target_bir_lowering=False, num_devices=1)
    build(nc, Declared(nc, arrays))
    r = run_bass_kernel_spmd(nc, [{f"in_{k}": v for k, v in arrays.items()}], core_ids=[0])
    y = r.results[0]["out_y"]
    return y.transpose(0, 3, 2, 1).reshape(BATCHES, S, HIDDEN)
```

```python
import concourse.bass as bass
from concourse import mybir
from contextlib import ExitStack

FP32 = mybir.dt.float32
FP32R = mybir.dt.float32r
ALU = mybir.AluOpType
ACT = mybir.ActivationFunctionType
AX = mybir.AxisListType

P = 128
S = 128
BATCHES = 16
HIDDEN = 1024
KT = HIDDEN // P
HEADS, KV_HEADS, HEAD_DIM = 32, 8, 128
GROUPS = KV_HEADS
GH = HEADS // KV_HEADS
TB = 4
BLOCKS = BATCHES // TB
TOK = TB * S
EXPERTS, RANK, TOPK = 64, 16, 16
LORA = EXPERTS * RANK
ALPHA_OVER_RANK = 32.0 / 16
EPS = 1e-5
UNIT = 1024
RING = 5
FFN_RING = 4
UPG = 10
FIRST_UNITS = 6
UPB = UPG * GROUPS
LOWEST = -3.0e38


def split_product(nc, out, pairs, first, last):
    done = None
    for i, (w_hi, w_lo, m_hi, m_lo) in enumerate(pairs):
        s, e = first and i == 0, last and i == len(pairs) - 1
        nc.tensor.matmul(out, w_hi, m_hi, start=s, stop=False)
        nc.tensor.matmul(out, w_hi, m_lo, start=False, stop=False)
        done = nc.tensor.matmul(out, w_lo, m_hi, start=False, stop=e)
    return done


class Arena:

    def __init__(self, nc, tag):
        self.nc, self.tag = nc, tag
        self.start = self.at = -(-nc.sbuf_base // 64) * 64

    def put(self, name, shape, dtype=FP32, over=None):
        size = 4
        for n in shape[1:]:
            size *= n
        at = self.at if over is None else over
        t = self.nc.alloc_sbuf_tensor_at(f"{self.tag}_{name}", shape, dtype, offset=at)
        if over is None:
            self.at += -(-size // 64) * 64
        return t

    def skip_to(self, size):
        assert self.at <= self.start + size
        self.at = self.start + size

    def pair(self, name, shape, raw=False):
        hi = self.put(name + "_hi", shape, FP32R)
        at = self.at
        lo = self.put(name + "_lo", shape, FP32R)
        return (hi, lo, self.put(name + "_raw", shape, FP32, over=at)) if raw else (hi, lo)


CTX_BYTES = XN_BYTES = 2 * KT * TOK * 4


class Early:

    def __init__(self, nc, sem):
        self.arena = a = Arena(nc, "ff")
        self.ring = [a.pair(f"ring{s}", [P, UNIT], raw=True) for s in range(FFN_RING)]
        a.skip_to(CTX_BYTES)
        self.x2_res = a.put("x2_res", [P, KT, TOK])
        self.router = a.pair("router", [P, KT, P], raw=True)
        self.expand_in = a.put("expand_in", [P, KT, P])
        self.ident = a.put("ident", [P, P])
        self.eps, self.gate_in = a.put("eps", [P, 1]), a.put("gate_in", [P, 1])
        a.skip_to(CTX_BYTES + XN_BYTES)
        self.x2_ln = a.put("x2_ln", [P, KT, TOK])
        self.const_in, self.x2_ln_in, self.x2_res_in = sem("f_const_in"), sem("x2_ln_in"), sem("x2_res_in")
        self.unit_raw = [sem(f"f_unit_raw{s}") for s in range(FFN_RING)]

    def load_over_context_and_rows(self, sp, d):
        sp.dma_start(self.x2_ln[:, :, :], d.x2t[0]).then_inc(self.x2_ln_in, 16)
        for c in range(FFN_RING):
            sp.dma_start(self.ring[c][2][:, :], d.w_a[c]).then_inc(self.unit_raw[c], 16)

    def load_over_layernorm(self, sp, d):
        sp.dma_start(self.ident[:, :], d.ident).then_inc(self.const_in, 16)
        sp.dma_start(self.gate_in[:, :], d.g_f).then_inc(self.const_in, 16)
        sp.dma_start(self.eps[:, :], d.eps).then_inc(self.const_in, 16)
        sp.dma_start(self.expand_in[:, :, :], d.expand).then_inc(self.const_in, 16)
        sp.dma_start(self.router[2][:, :, :], d.w_r.rearrange("p (k o) -> p k o", k=KT)).then_inc(self.const_in, 16)
        sp.dma_start(self.x2_res[:, :, :], d.x2t[0]).then_inc(self.x2_res_in, 16)


def attention_phase(nc, ctx, sem, psum, d, early):
    a = Arena(nc, "at")
    cx_hi, cx_lo, cx_raw = a.pair("ctx", [P, KT, TOK], raw=True)
    a.skip_to(CTX_BYTES)
    xn_hi, xn_lo = a.pair("xn", [P, KT, TOK])
    a.skip_to(CTX_BYTES + XN_BYTES)
    x_rows = a.put("x_rows", [P, TB, HIDDEN])
    ring = [a.pair(f"ring{s}", [P, UNIT], raw=True) for s in range(RING)]
    acc = a.put("acc", [P, KT, TOK])
    vn_hi, vn_lo = a.pair("v_new", [P, TB, HEAD_DIM])
    vc_hi, vc_lo = a.pair("v_cur", [P, TB, HEAD_DIM])
    k_sb = a.put("k_sb", [P, TB, HEAD_DIM])
    k_n = a.put("k_n", [P, TB, HEAD_DIM])
    kt_sb = a.put("kt_sb", [P, TB, S])
    qt = [a.put(f"qt{i}", [P, TB, S]) for i in range(2)]
    sm = a.put("scores", [P, TB, S])
    pr = a.put("probs", [P, TB, S])
    pt_hi, pt_lo = a.pair("pt", [P, TB, GH, S])
    ot_hi, ot_lo = a.pair("ot", [P, GH, TB, S])
    mask = a.put("mask", [P, S])
    ident = a.put("ident", [P, P])
    k_sq = a.put("k_squares", [P, TB, HEAD_DIM])
    nw = a.put("norm_weights", [P, 2])
    kw = a.put("k_weight", [P, 1])
    gx = a.put("gate_in", [P, 1])
    tgx = a.put("gate", [P, 1])
    eps = a.put("eps", [P, 1])
    stats = a.put("stats", [P, TB, 2, 6])
    mv = a.put("mean_var", [P, TB, 2])
    x_ln, x_seed, x_v, x_t, x_rstd = (a.put("x_" + k, [P, TB]) for k in ("ln", "seed", "v", "t", "rstd"))
    k_ss, k_ln, k_seed, k_v, k_t, k_rstd = (a.put("k_" + k, [P, TB]) for k in ("ss", "ln", "seed", "v", "t", "rstd"))
    q_ss, q_ln, q_seed, q_v, q_t, q_rstd = (a.put("q_" + k, [P, TB]) for k in ("ss", "ln", "seed", "v", "t", "rstd"))
    nmax = a.put("neg_max", [P, TB])
    rsum = a.put("row_sum", [P, TB])
    rinv = a.put("row_inv", [P, TB])
    assert a.at <= nc.sbuf_top, a.at

    bank_a, bank_b, bank_o0, bank_o1, bank_s, bank_t, bank_x, bank_v = psum
    proj = (bank_a, bank_b)

    const_in = sem("const_in")
    unit_raw = [sem(f"unit_raw{s}") for s in range(RING)]
    ctx_raw = [sem(f"ctx_raw{half}") for half in range(2)]
    first_ctx_raw = [sem(f"first_ctx_raw{i}") for i in range(8)]
    first_rows_raw = [sem(f"first_rows_raw{t}") for t in range(TB)]
    rows_raw, acc_raw, x2t_out = sem("rows_raw"), sem("acc_raw"), sem("x2t_out")
    gate_tanh, eps_set, kw_set = sem("gate_tanh"), sem("eps_set"), sem("kw_set")
    unit_hi, unit_lo, ctx_hi, ctx_lo = sem("unit_hi"), sem("unit_lo"), sem("ctx_hi"), sem("ctx_lo")
    row_stats, row_aggr, row_ln, row_seed, row_step, row_norm = (
        sem(k) for k in ("row_stats", "row_aggr", "row_ln", "row_seed", "row_step", "row_norm"))
    xt_done, xn_hi_done, xn_lo_done = sem("xt_done"), sem("xn_hi_done"), sem("xn_lo_done")
    kv_done, q_done, t1_done, s_done, pt_done = sem("kv_done"), sem("q_done"), sem("t1_done"), sem("s_done"), sem("pt_done")
    pv_done, o_done, kt_done = sem("pv_done"), sem("o_done"), sem("kt_done")
    k_squared, v_hi_done, k_copied, v_lo_done, k_seeded, kt_copied = (
        sem("k_squared"), sem("v_hi_done"), sem("k_copied"), sem("v_lo_done"), sem("k_seeded"), sem("kt_copied"))
    q_copied, q_squared, q_seeded = sem("q_copied"), sem("q_squared"), sem("q_seeded")
    rstd_step, k_scaled, v_moved = sem("rstd_step"), sem("k_scaled"), sem("v_moved")
    s_masked, s_max, p_exp, p_inv, p_norm = sem("s_masked"), sem("s_max"), sem("p_exp"), sem("p_inv"), sem("p_norm")
    pt_hi_done, pt_lo_done, ot_hi_done, ot_lo_done, acc_add = (
        sem("pt_hi_done"), sem("pt_lo_done"), sem("ot_hi_done"), sem("ot_lo_done"), sem("acc_add"))
    act_step = sem("act_step")
    vector_waited, pool_waited = sem("vector_waited"), sem("pool_waited")

    CONSTS = 5
    block = ctx.enter_context(nc.Block())

    KEYS, QUERIES = 0, 1

    def newton_after(n, item):
        return n * 25 + 5 * (item + 1)

    SPLIT_FIRST = {0: 3, 1: 4, 2: 5, 7: 6, 8: 7, 9: 8}
    SPLIT_LATER = {i: i + 3 + FIRST_UNITS - UPG for i in range(10)}
    xt_banks = (bank_v, bank_t, bank_o0, bank_o1)

    def ctx_part(t, half, i):
        return t[:, 2 * i:2 * i + 2, half * 2 * S:(half + 1) * 2 * S]

    @block.sync
    def _(sp):
        def unit(slot, src):
            sp.dma_start(ring[slot][2][:, :], src).then_inc(unit_raw[slot], 16)

        def load_ctx(b):
            for half in range(2):
                tok = slice(half * 2 * S, (half + 1) * 2 * S)
                sp.dma_start(cx_raw[:, :, tok], d.ctx_t[b, :, :, tok]).then_inc(ctx_raw[half], 16)

        def first_ctx(half, parts):
            for i in parts:
                sp.dma_start(ctx_part(cx_raw, half, i), ctx_part(d.ctx_t[0], half, i)).then_inc(first_ctx_raw[4 * half + i], 16)

        def x2_out(b, i):
            sp.wait_ge(acc_add, (b + 1) * (8 * GROUPS) + (2 * i + 2))
            sp.dma_start(d.x2t[b, :, 2 * i:2 * i + 2, :], acc[:, 2 * i:2 * i + 2, :]).then_inc(x2t_out, 16)

        def x_in(b, i):
            sp.wait_ge(x2t_out, b * 64 + 16 * (i + 1))
            sp.dma_start(acc[:, 2 * i:2 * i + 2, :], d.x_t[b + 1, :, 2 * i:2 * i + 2, :]).then_inc(acc_raw, 16)

        def group(b, g, o_of, first=False, second=False, last=False):
            n = b * GROUPS + g
            sp.wait_ge(q_done, n * 4 - 1)
            unit(1, d.w_kv[g, 0])
            unit(2, d.w_kv[g, 1])
            if second:
                x_in(b - 1, 1)
                x2_out(b - 1, 2)
            sp.wait_ge(q_done, n * 4)
            unit(3, d.w_q[g, 0])
            unit(4, d.w_o[o_of, 0])
            if second:
                x_in(b - 1, 2)
                x2_out(b - 1, 3)
                x_in(b - 1, 3)
            sp.wait_ge(kv_done, n * 2 + 1)
            unit(0, d.w_q[g, 1])
            sp.wait_ge(kv_done, n * 2 + 2)
            unit(1, d.w_o[o_of, 1])
            unit(2, d.w_q[g, 2])
            sp.wait_ge(q_done, n * 4 + 1)
            unit(3, d.w_o[o_of, 2])
            if last:
                load_ctx(b + 1)
            sp.wait_ge(o_done, n * 8 - 6)
            unit(4, d.w_q[g, 3])
            if first:
                x2_out(b - 1, 0)
            sp.wait_ge(q_done, n * 4 + 2)
            unit(0, d.w_o[o_of, 3])
            if first:
                x_in(b - 1, 0)
                x2_out(b - 1, 1)

        unit(0, d.w_kv[0, 0])
        first_ctx(0, range(0, 2))
        unit(1, d.w_kv[0, 1])
        first_ctx(0, range(2, 4))
        first_ctx(1, range(4))
        sp.dma_start(gx[:, :], d.g_x).then_inc(const_in, 16)
        sp.dma_start(nw[:, :], d.norm_w).then_inc(const_in, 16)
        sp.dma_start(ident[:, :], d.ident).then_inc(const_in, 16)
        sp.dma_start(mask[:, :], d.mask).then_inc(const_in, 16)
        sp.dma_start(eps[:, :], d.eps).then_inc(const_in, 16)
        for t in range(TB):
            sp.dma_start(x_rows[:, t, :], d.x_rows[0, :, t, :]).then_inc(first_rows_raw[t], 16)
        unit(2, d.w_q[0, 0])
        unit(3, d.w_q[0, 1])
        unit(4, d.w_q[0, 2])
        for i in range(4):
            sp.dma_start(acc[:, 2 * i:2 * i + 2, :], d.x_t[0, :, 2 * i:2 * i + 2, :]).then_inc(acc_raw, 16)
        sp.wait_ge(kv_done, 2)
        unit(0, d.w_q[0, 3])
        group(0, 1, 0)
        with sp.Fori(0, BLOCKS - 1) as b:
            sp.wait_ge(xt_done, b * KT + KT)
            sp.dma_start(x_rows[:, :, :], d.x_rows[b + 1]).then_inc(rows_raw, 16)
            with sp.Fori(2, GROUPS - 1) as g:
                group(b, g, g - 1)
            group(b, GROUPS - 1, GROUPS - 2, last=True)
            group(b + 1, 0, GROUPS - 1, first=True)
            group(b + 1, 1, 0, second=True)
        b = BLOCKS - 1
        with sp.Fori(2, GROUPS) as g:
            group(b, g, g - 1)
        n = BLOCKS * GROUPS
        early.load_over_context_and_rows(sp, d)
        sp.wait_ge(q_done, n * 4 - 1)
        unit(1, d.w_o[GROUPS - 1, 0])
        unit(2, d.w_o[GROUPS - 1, 1])
        sp.wait_ge(q_done, n * 4)
        unit(3, d.w_o[GROUPS - 1, 2])
        unit(4, d.w_o[GROUPS - 1, 3])
        early.load_over_layernorm(sp, d)
        for i in range(4):
            x2_out(b, i)
        sp.wait_ge(x2t_out, BLOCKS * 64)

    @block.tensor
    def _(pe):
        def w_ready(b, g, c):
            pe.wait_ge(unit_lo, b * UPB + g * UPG + (c + 1))
            return ring[c % RING]

        def keys_values(n, half, units, ctx_before=None, second_unit_later=False):
            for t in (2 * half, 2 * half + 1):
                tok = slice(t * S, t * S + S)
                out = proj[half][:, (t % 2) * 256:(t % 2) * 256 + 256]
                for kt in range(KT):
                    if ctx_before is not None and t % 2 == 0 and kt % 2 == 0:
                        pe.wait_ge(ctx_lo, ctx_before + (half * 4 + kt // 2 + 1))
                    if second_unit_later and t == 0 and kt == 4:
                        units.append(w_ready(0, 0, 1))
                    w_hi, w_lo, _ = units[kt // 4]
                    cols = slice((kt % 4) * 256, (kt % 4) * 256 + 256)
                    done = split_product(nc, out, [(cx_hi[:, kt, tok], cx_lo[:, kt, tok], w_hi[:, cols], w_lo[:, cols])],
                                         kt == 0, kt == KT - 1)
            done.then_inc(kv_done, 1)

        def query(j, w, xn_before=None):
            for kt in range(KT):
                if xn_before is not None:
                    pe.wait_ge(xn_lo_done, xn_before + (kt + 1))
                cols = slice(kt * P, kt * P + P)
                done = split_product(nc, proj[j % 2][:, :], [(w[0][:, cols], w[1][:, cols], xn_hi[:, kt, :], xn_lo[:, kt, :])],
                                     kt == 0, kt == KT - 1)
            done.then_inc(q_done, 1)

        def query_rows(n, j):
            pe.wait_ge(q_copied, n * 4 + (j + 1))
            if j:
                pe.wait_ge(q_squared, n * 4 + j)
            for t in range(TB):
                done = nc.tensor.transpose(bank_t[:, t * S:t * S + S], qt[j % 2][:, t, :], ident[:, :])
            done.then_inc(t1_done, 1)

        def key_columns(n):
            pe.wait_ge(k_scaled, n + 1)
            for t in range(TB):
                done = nc.tensor.transpose(bank_x[:, t * S:t * S + S], k_n[:, t, :], ident[:, :])
            done.then_inc(kt_done, 1)

        def scores(n, j):
            if j == 0:
                pe.wait_ge(kt_copied, n + 1)
            else:
                pe.wait_ge(s_masked, n * 4 + j)
            for t in range(TB):
                done = nc.tensor.matmul(bank_s[:, t * S:t * S + S], qt[j % 2][:, t, :], kt_sb[:, t, :], start=True, stop=True)
            done.then_inc(s_done, 1)

        def probs_columns(n, j):
            pe.wait_ge(p_norm, n * 4 + (j + 1))
            if j:
                pe.wait_ge(pt_lo_done, n * 4 + j)
            for t in range(TB):
                done = nc.tensor.transpose(bank_x[:, t * S:t * S + S], pr[:, t, :], ident[:, :])
            done.then_inc(pt_done, 1)

        def weighted_values(n, xn_before=None):
            pe.wait_ge(pt_lo_done, n * 4 + 4)
            for t, bank in enumerate((bank_v, bank_t, bank_o0, bank_o1)):
                if xn_before is not None:
                    pe.wait_ge(xn_lo_done, xn_before + (t + 5))
                if t == 0:
                    pe.wait_ge(v_moved, n + 1)
                if t == 2:
                    pe.wait_ge(acc_add, n * 8 + 8)
                done = split_product(nc, bank[:, :], [(
                    vc_hi[:, t, :], vc_lo[:, t, :],
                    pt_hi[:, t, :, :].rearrange("p h q -> p (h q)"), pt_lo[:, t, :, :].rearrange("p h q -> p (h q)"))],
                    True, True)
                done.then_inc(pv_done, 1)

        def output(n, c, w):
            bank = (bank_o0, bank_o1)[c % 2]
            if c < 2:
                pe.wait_ge(ot_lo_done, n * 4 + 4)
            else:
                pe.wait_ge(acc_add, n * 8 + (c + 7))
            pairs = []
            for h in range(GH):
                cols = slice((c % 2) * 512 + h * P, (c % 2) * 512 + h * P + P)
                pairs.append((w[0][:, cols], w[1][:, cols],
                              ot_hi[:, h, :, :].rearrange("p t q -> p (t q)"), ot_lo[:, h, :, :].rearrange("p t q -> p (t q)")))
            split_product(nc, bank[:, :], pairs, True, True).then_inc(o_done, 1)

        def group(b, g, first=False, only=False):
            n = b * GROUPS + g
            c = 0 if only else FIRST_UNITS - UPG
            new_ctx = b * KT if first else None
            new_xn = b * KT if first else None
            if first and not only:
                rows_transposed(b, n, range(0, 2), only)
            units = [w_ready(b, g, c)]
            if not only:
                units.append(w_ready(b, g, c + 1))
            keys_values(n, 0, units, new_ctx, only)
            if not only:
                probs_columns(n - 1, 3)
            if first and not only:
                rows_transposed(b, n, range(2, 6), only)
            keys_values(n, 1, units, new_ctx)
            if first:
                rows_transposed(b, n, range(0 if only else 6, 8), only)
            if not only:
                weighted_values(n - 1, new_xn)
            pe.wait_ge(v_lo_done, n * 2 + 1)
            for j in range(GH):
                k = c + 2 + (j if only else 2 * j)
                if j == 1:
                    pe.wait_ge(v_lo_done, n * 2 + 2)
                query(j, w_ready(b, g, k), new_xn if j == 0 else None)
                if not only:
                    w = w_ready(b, g, k + 1)
                    output(n - 1, 2 * j, w)
                query_rows(n, j)
                if j == 0:
                    key_columns(n)
                if not only and j < 3:
                    output(n - 1, 2 * j + 1, w)
                if j:
                    probs_columns(n, j - 1)
                scores(n, j)
            if not only:
                output(n - 1, 7, w)

        def rows_transposed(b, n, kts, only):
            for kt in kts:
                if kt == 0 and only:
                    pe.wait_ge(const_in, 16 * CONSTS)
                if kt == 0:
                    pe.wait_ge(row_norm, b * TB + TB)
                if not only and kt == 1:
                    pe.wait_ge(q_squared, n * 4)
                if not only and kt in (2, 3):
                    pe.wait_ge(acc_add, n * 8 + (kt - 3))
                if kt >= 4:
                    pe.wait_ge(xn_lo_done, b * KT + (kt - 3))
                for t in range(TB):
                    done = nc.tensor.transpose(xt_banks[kt % 4][:, t * S:t * S + S], x_rows[:, t, kt * P:kt * P + P], ident[:, :])
                done.then_inc(xt_done, 1)

        group(0, 0, first=True, only=True)
        with pe.Fori(0, BLOCKS - 1) as b:
            with pe.Fori(1, GROUPS) as g:
                group(b, g)
            group(b + 1, 0, first=True)
        with pe.Fori(1, GROUPS) as g:
            group(BLOCKS - 1, g)
        n = BLOCKS * GROUPS - 1
        probs_columns(n, 3)
        weighted_values(n)
        for c in range(8):
            if c % 2 == 0:
                w = w_ready(BLOCKS - 1, GROUPS, c // 2 - 4)
            output(n, c, w)

    @block.scalar
    def _(act):
        def split(b, g, c):
            act.wait_ge(unit_raw[c % RING], b * (16 * UPB // RING) + g * (16 * UPG // RING) + 16 * (c // RING + 1))
            nc.scalar.copy(ring[c % RING][0][:, :], ring[c % RING][2][:, :]).then_inc(unit_hi, 1)

        def values_half(n, half):
            act.wait_ge(kv_done, n * 2 + (half + 1))
            bank = proj[half][:, :].rearrange("p (t c) -> p t c", c=256)
            for i in range(2):
                last = nc.scalar.activation(k_sq[:, 2 * half + i, :], bank[:, i, 0:128], ACT.Square,
                                            accum_out=k_ss[:, 2 * half + i:2 * half + i + 1])
            last.then_inc(k_squared, 1)
            nc.scalar.copy(vn_hi[:, 2 * half:2 * half + 2, :], bank[:, :, 128:256]).then_inc(v_hi_done, 1)

        def probs_high(n, j):
            act.wait_ge(pt_done, n * 4 + (j + 1))
            nc.scalar.copy(pt_hi[:, :, j, :], bank_x[:, :].rearrange("p (t q) -> p t q", q=S)).then_inc(pt_hi_done, 1)

        def heads_high(n):
            for t, bank in enumerate((bank_v, bank_t, bank_o0, bank_o1)):
                act.wait_ge(pv_done, n * 4 + (t + 1))
                nc.scalar.copy(ot_hi[:, :, t, :], bank[:, :].rearrange("p (h q) -> p h q", q=S)).then_inc(ot_hi_done, 1)

        def query_copied(n, j):
            act.wait_ge(q_done, n * 4 + (j + 1))
            nc.scalar.copy(qt[j % 2][:, :, :], proj[j % 2][:, :].rearrange("p (t q) -> p t q", q=S)).then_inc(q_copied, 1)

        def query_squares(n, j):
            act.wait_ge(t1_done, n * 4 + (j + 1))
            for t in range(TB):
                last = nc.scalar.activation(bank_t[:, t * S:t * S + S], bank_t[:, t * S:t * S + S], ACT.Square, accum_out=q_ss[:, t:t + 1])
            last.then_inc(q_squared, 1)
            act.wait_ge(q_squared, n * 4 + (j + 1))
            nc.scalar.activation(q_ln[:, :], q_ss[:, :], ACT.Ln, bias=eps[:, :], scale=1.0 / HEAD_DIM).then_inc(act_step, 1)
            act.wait_ge(act_step, n * 5 + (j + 2))
            nc.scalar.activation(q_seed[:, :], q_ln[:, :], ACT.Exp, scale=-0.5).then_inc(q_seeded, 1)

        def ctx_high(b, half, parts=range(4), is_first=False):
            if not is_first:
                act.wait_ge(ctx_raw[half], b * 16)
            for i in parts:
                if is_first:
                    act.wait_ge(first_ctx_raw[4 * half + i], 16)
                nc.scalar.copy(ctx_part(cx_hi, half, i), ctx_part(cx_raw, half, i)).then_inc(ctx_hi, 1)

        def row_seeds(b):
            act.wait_ge(row_aggr, b * TB + TB)
            nc.scalar.activation(x_ln[:, :], mv[:, :, 1], ACT.Ln, bias=eps[:, :]).then_inc(row_ln, 1)
            act.wait_ge(row_ln, b + 1)
            nc.scalar.activation(x_seed[:, :], x_ln[:, :], ACT.Exp, scale=-0.5).then_inc(row_seed, 1)

        def columns_high(b, kts):
            for kt in kts:
                act.wait_ge(xt_done, b * KT + (kt + 1))
                nc.scalar.copy(xn_hi[:, kt, :], xt_banks[kt % 4][:, :]).then_inc(xn_hi_done, 1)

        def exps(n, j):
            act.wait_ge(s_max, n * 4 + (j + 1))
            for t in range(TB):
                last = nc.scalar.activation(pr[:, t, :], sm[:, t, :], ACT.Exp, bias=nmax[:, t:t + 1], accum_out=rsum[:, t:t + 1])
            last.then_inc(p_exp, 1)

        def group(b, g, first=False, only=False, last=False):
            n = b * GROUPS + g
            where = SPLIT_FIRST if only else SPLIT_LATER

            def split_at(place):
                if place in where:
                    split(b, g, where[place])

            if first and not only:
                columns_high(b, range(0, 2))
            split_at(0)
            values_half(n, 0)
            if not only:
                probs_high(n - 1, 3)
            if first and not only:
                columns_high(b, range(2, 6))
            split_at(1)
            values_half(n, 1)
            act.wait_ge(k_squared, n * 2 + 2)
            nc.scalar.activation(k_ln[:, :], k_ss[:, :], ACT.Ln, bias=eps[:, :], scale=1.0 / HEAD_DIM).then_inc(act_step, 1)
            act.wait_ge(act_step, n * 5 + 1)
            nc.scalar.activation(k_seed[:, :], k_ln[:, :], ACT.Exp, scale=-0.5).then_inc(k_seeded, 1)
            if last:
                row_seeds(b + 1)
            if first:
                columns_high(b, range(0 if only else 6, 8))
            if not only:
                heads_high(n - 1)
            query_copied(n, 0)
            split_at(2)
            query_squares(n, 0)
            act.wait_ge(kt_done, n + 1)
            nc.scalar.activation(kt_sb[:, :, :], bank_x[:, :].rearrange("p (t q) -> p t q", q=S), ACT.Copy,
                                 scale=kw[:, :]).then_inc(kt_copied, 1)
            split_at(3)
            exps(n, 0)
            for j in (1, 2, 3):
                query_copied(n, j)
                split_at(2 * j + 2)
                query_squares(n, j)
                probs_high(n, j - 1)
                split_at(2 * j + 3)
                exps(n, j)
                if last and j < 3:
                    ctx_high(b + 1, j - 1)

        split(0, 0, 0)
        ctx_high(0, 0, range(0, 2), True)
        split(0, 0, 1)
        ctx_high(0, 0, range(2, 4), True)
        ctx_high(0, 1, range(4), True)
        act.wait_ge(const_in, 16 * CONSTS)
        nc.scalar.activation(tgx[:, :], gx[:, :], ACT.Tanh).then_inc(gate_tanh, 1)
        act.preload_act_table_set("natural_log_exp_and_others")
        row_seeds(0)
        split(0, 0, 2)
        group(0, 0, first=True, only=True)
        with act.Fori(0, BLOCKS - 1) as b:
            with act.Fori(1, GROUPS - 1) as g:
                group(b, g)
            group(b, GROUPS - 1, last=True)
            group(b + 1, 0, first=True)
        with act.Fori(1, GROUPS) as g:
            group(BLOCKS - 1, g)
        n = BLOCKS * GROUPS - 1
        probs_high(n, 3)
        split(BLOCKS - 1, GROUPS, -1)
        heads_high(n)

    @block.vector
    def _(dve):
        def split(b, g, c):
            hi, lo, raw = ring[c % RING]
            dve.wait_ge(unit_hi, b * UPB + g * UPG + (c + 1))
            nc.vector.tensor_tensor(lo[:, :], raw[:, :], hi[:, :].bitcast(FP32), ALU.subtract).then_inc(unit_lo, 1)

        def low(out, whole, hi):
            return nc.vector.tensor_tensor(out, whole, hi.bitcast(FP32), ALU.subtract)

        def alone():
            dve.sem_inc(vector_waited, 1)

        def values_half(n, half):
            bank = proj[half][:, :].rearrange("p (t c) -> p t c", c=256)
            dve.wait_ge(v_hi_done, n * 2 + (half + 1))
            nc.vector.tensor_copy(k_sb[:, 2 * half:2 * half + 2, :], bank[:, :, 0:128]).then_inc(k_copied, 1)
            low(vn_lo[:, 2 * half:2 * half + 2, :], bank[:, :, 128:256],
                vn_hi[:, 2 * half:2 * half + 2, :]).then_inc(v_lo_done, 1)

        def probs_low(n, j):
            dve.wait_ge(pt_hi_done, n * 4 + (j + 1))
            low(pt_lo[:, :, j, :], bank_x[:, :].rearrange("p (t q) -> p t q", q=S), pt_hi[:, :, j, :]).then_inc(pt_lo_done, 1)

        def heads_low(n):
            for t, bank in enumerate((bank_v, bank_t, bank_o0, bank_o1)):
                dve.wait_ge(ot_hi_done, n * 4 + (t + 1))
                low(ot_lo[:, :, t, :], bank[:, :].rearrange("p (h q) -> p h q", q=S), ot_hi[:, :, t, :]).then_inc(ot_lo_done, 1)

        def add_output(n, c):
            dve.wait_ge(o_done, n * 8 + (c + 1))
            nc.vector.scalar_tensor_tensor(acc[:, c, :], (bank_o0, bank_o1)[c % 2][:, :], tgx[:, :], acc[:, c, :],
                                           ALU.mult, ALU.add).then_inc(acc_add, 1)

        def softmax_max(n, j):
            dve.wait_ge(s_done, n * 4 + (j + 1))
            dve.wait_ge(rstd_step, newton_after(n, QUERIES + j))
            for t in range(TB):
                last = nc.vector.scalar_tensor_tensor(sm[:, t, :], bank_s[:, t * S:t * S + S], q_rstd[:, t:t + 1], mask[:, :],
                                                      ALU.mult, ALU.add)
            last.then_inc(s_masked, 1)
            dve.wait_ge(s_masked, n * 4 + (j + 1))
            nc.vector.tensor_reduce(nmax[:, :], sm[:, :, :], AX.X, ALU.max, negate=True).then_inc(s_max, 1)

        def softmax_norm(n, j):
            dve.wait_ge(p_exp, n * 4 + (j + 1))
            nc.vector.reciprocal(rinv[:, :], rsum[:, :]).then_inc(p_inv, 1)
            dve.wait_ge(p_inv, n * 4 + (j + 1))
            nc.vector.tensor_tensor(pr[:, :, :], pr[:, :, :], rinv[:, :].unsqueeze(2).to_broadcast([P, TB, S]),
                                    ALU.mult).then_inc(p_norm, 1)

        def context_low(b, half, parts=range(4)):
            for i in parts:
                dve.wait_ge(ctx_hi, b * KT + (half * 4 + i + 1))
                low(ctx_part(cx_lo, half, i), ctx_part(cx_raw, half, i), ctx_part(cx_hi, half, i)).then_inc(ctx_lo, 1)

        def row_statistics(b, t, is_first=False):
            if is_first:
                dve.wait_ge(first_rows_raw[t], 16)
                alone()
            elif t == 0:
                dve.wait_ge(rows_raw, b * 16)
                alone()
            for i in range(2):
                last = nc.vector.bn_stats(stats[:, t, i, :], x_rows[:, t, i * 512:i * 512 + 512])
            last.then_inc(row_stats, 1)
            dve.wait_ge(row_stats, b * TB + (t + 1))
            alone()
            nc.vector.bn_aggr(mv[:, t, :], stats[:, t, :, :].rearrange("p i s -> p (i s)")).then_inc(row_aggr, 1)

        def normalise_rows(b, t):
            dve.wait_ge(row_step, b * 5 + 5)
            nc.vector.tensor_scalar(x_rows[:, t, :], x_rows[:, t, :], mv[:, t, 0:1], x_rstd[:, t:t + 1],
                                    ALU.subtract, ALU.mult).then_inc(row_norm, 1)

        def columns_low(b, kts):
            for kt in kts:
                dve.wait_ge(xn_hi_done, b * KT + (kt + 1))
                low(xn_lo[:, kt, :], xt_banks[kt % 4][:, :], xn_hi[:, kt, :]).then_inc(xn_lo_done, 1)

        def group(b, g, first=False, only=False, last=False):
            n = b * GROUPS + g
            where = SPLIT_FIRST if only else SPLIT_LATER

            def split_at(place):
                if place in where:
                    split(b, g, where[place])

            if last:
                row_statistics(b + 1, 0)
                row_statistics(b + 1, 1)
            if first and not only:
                columns_low(b, range(0, 2))
            split_at(0)
            values_half(n, 0)
            if not only:
                probs_low(n - 1, 3)
            if first and not only:
                columns_low(b, range(2, 6))
            split_at(1)
            if last:
                row_statistics(b + 1, 2)
                row_statistics(b + 1, 3)
            values_half(n, 1)
            if first:
                columns_low(b, range(0 if only else 6, 8))
            if not only:
                heads_low(n - 1)
            split_at(2)
            if not only:
                dve.wait_ge(acc_raw, b * 64 + 64 if not first else b * 64)
                add_output(n - 1, 0)
                add_output(n - 1, 1)
            softmax_max(n, 0)
            split_at(3)
            softmax_norm(n, 0)
            for j in (1, 2, 3):
                if not only:
                    add_output(n - 1, 2 * j)
                    if j < 3:
                        add_output(n - 1, 2 * j + 1)
                split_at(2 * j + 2)
                probs_low(n, j - 1)
                softmax_max(n, j)
                split_at(2 * j + 3)
                softmax_norm(n, j)
                if last and j < 3:
                    normalise_rows(b + 1, 2 * j - 2)
                    context_low(b + 1, j - 1)
                    normalise_rows(b + 1, 2 * j - 1)
            if not only:
                add_output(n - 1, 7)

        split(0, 0, 0)
        context_low(0, 0, range(0, 2))
        split(0, 0, 1)
        context_low(0, 0, range(2, 4))
        context_low(0, 1)
        for t in range(TB):
            row_statistics(0, t, True)
        dve.wait_ge(const_in, 16 * CONSTS)
        nc.vector.tensor_scalar(kw[:, :], nw[:, 0:1], nw[:, 1:2], float(HEAD_DIM) ** -0.5, ALU.mult, ALU.mult).then_inc(kw_set, 1)
        dve.wait_ge(kw_set, 1)
        dve.wait_ge(gate_tanh, 1)
        nc.vector.tensor_copy(rinv[:, 0:1], tgx[:, :]).then_inc(acc_add, 8)
        for t in range(TB):
            normalise_rows(0, t)
        split(0, 0, 2)
        group(0, 0, first=True, only=True)
        with dve.Fori(0, BLOCKS - 1) as b:
            with dve.Fori(1, GROUPS - 1) as g:
                group(b, g)
            group(b, GROUPS - 1, last=True)
            group(b + 1, 0, first=True)
        with dve.Fori(1, GROUPS) as g:
            group(BLOCKS - 1, g)
        n = BLOCKS * GROUPS - 1
        probs_low(n, 3)
        split(BLOCKS - 1, GROUPS, -1)
        heads_low(n)
        for c in range(8):
            add_output(n, c)

    @block.gpsimd
    def _(pool):
        def alone():
            pool.sem_inc(pool_waited, 1)

        def newton(ss, scale, seed, v, t, out, step, after):
            nc.gpsimd.tensor_scalar(v[:, :], ss, scale, EPS, ALU.mult, ALU.add).then_inc(step, 1)
            nc.gpsimd.tensor_tensor(t[:, :], seed[:, :], seed[:, :], ALU.mult).then_inc(step, 1)
            pool.wait_ge(step, after - 3)
            nc.gpsimd.tensor_tensor(t[:, :], t[:, :], v[:, :], ALU.mult).then_inc(step, 1)
            pool.wait_ge(step, after - 2)
            alone()
            nc.gpsimd.tensor_scalar(t[:, :], t[:, :], -0.5, 1.5, ALU.mult, ALU.add).then_inc(step, 1)
            pool.wait_ge(step, after - 1)
            nc.gpsimd.tensor_tensor(out[:, :], t[:, :], seed[:, :], ALU.mult).then_inc(step, 1)

        def rows(b):
            pool.wait_ge(row_seed, b + 1)
            alone()
            newton(mv[:, :, 1], 1.0, x_seed, x_v, x_t, x_rstd, row_step, b * 5 + 5)

        def group(b, g, last=False):
            n = b * GROUPS + g
            pool.wait_ge(k_seeded, n + 1)
            alone()
            after = newton_after(n, KEYS)
            newton(k_ss[:, :], 1.0 / HEAD_DIM, k_seed, k_v, k_t, k_rstd, rstd_step, after)
            pool.wait_ge(rstd_step, after)
            pool.wait_ge(k_copied, n * 2 + 2)
            nc.gpsimd.tensor_tensor(k_n[:, :, :], k_sb[:, :, :], k_rstd[:, :].unsqueeze(2).to_broadcast([P, TB, HEAD_DIM]),
                                    ALU.mult).then_inc(k_scaled, 1)
            if last:
                rows(b + 1)
            for j in range(GH):
                pool.wait_ge(q_seeded, n * 4 + (j + 1))
                alone()
                newton(q_ss[:, :], 1.0 / HEAD_DIM, q_seed, q_v, q_t, q_rstd, rstd_step, newton_after(n, QUERIES + j))
                if j == 0:
                    pool.wait_ge(v_lo_done, n * 2 + 2)
                    alone()
                    nc.gpsimd.tensor_copy(vc_hi[:, :, :], vn_hi[:, :, :].bitcast(FP32))
                    nc.gpsimd.tensor_copy(vc_lo[:, :, :], vn_lo[:, :, :].bitcast(FP32)).then_inc(v_moved, 1)

        rows(0)
        group(0, 0)
        with pool.Fori(0, BLOCKS - 1) as b:
            with pool.Fori(1, GROUPS - 1) as g:
                group(b, g)
            group(b, GROUPS - 1, last=True)
            group(b + 1, 0)
        with pool.Fori(1, GROUPS) as g:
            group(BLOCKS - 1, g)


def ffn_phase(nc, ctx, sem, psum, d, early):
    a = early.arena
    ring, x2_ln, x2_res, ident, eps, g_in = early.ring, early.x2_ln, early.x2_res, early.ident, early.eps, early.gate_in
    wr_hi, wr_lo, wr_raw = early.router
    expand_in = early.expand_in
    rows = a.put("rows", [P, TB, HIDDEN])
    xn_hi, xn_lo = a.pair("xn", [P, KT, TOK])
    hg_hi, hg_lo = a.pair("hg", [P, KT, TOK])
    expand = a.put("expand", [P, KT, P], FP32R)
    gt_hi, gt_lo = a.pair("gt", [P, TOK])
    sct = a.put("router_scores_t", [P, TB, S])
    sc, w1, w2, sel, ex = (a.put(k, [P, TB, EXPERTS]) for k in ("scores", "without8", "without16", "chosen", "exps"))
    gates = a.put("gates", [P, TB, P])
    m1, m2 = a.put("top8", [P, TB, 8]), a.put("next8", [P, TB, 8])
    g_nmax, g_sum, g_inv = a.put("g_neg_max", [P, TB]), a.put("g_sum", [P, TB]), a.put("g_inv", [P, TB])
    g_rep = [a.put(f"gates_of_ranks{i}", [P, TOK]) for i in range(2)]
    hg = [a.put(f"hg{i}", [P, TOK]) for i in range(2)]
    tg, tg2 = a.put("gate", [P, 1]), a.put("gate_scaled", [P, 1])
    stats, mv = a.put("stats", [P, TB, 2, 6]), a.put("mean_var", [P, TB, 2])
    ln, seed, nv, nt, rstd = (a.put("row_" + k, [P, TB]) for k in ("ln", "seed", "v", "t", "rstd"))
    assert a.at <= nc.sbuf_top, a.at

    bank_h, bank_e, bank_x = psum[0:4], psum[4:6], psum[6:8]
    prep_banks = (bank_x[0], bank_x[1], bank_e[0], bank_e[1])

    const_in, x2_ln_in, x2_res_in, unit_raw = early.const_in, early.x2_ln_in, early.x2_res_in, early.unit_raw
    y_out = sem("y_out")
    gate_tanh, gate_set = sem("f_gate_tanh"), sem("f_gate_set")
    unit_hi, unit_lo, router_hi, router_lo = sem("f_unit_hi"), sem("f_unit_lo"), sem("router_hi"), sem("router_lo")
    tt_done, row_stats, row_aggr, row_ln, row_seed, row_norm, rstd_step = (
        sem(k) for k in ("tt_done", "f_row_stats", "f_row_aggr", "row_ln", "f_row_seed", "f_row_norm", "f_rstd_step"))
    xt_done, xn_hi_done, xn_lo_done = sem("f_xt_done"), sem("f_xn_hi_done"), sem("f_xn_lo_done")
    r_done, sct_copied, st_done, gate_step, gate_max, gate_exp, gates_done = (
        sem(k) for k in ("r_done", "sct_copied", "st_done", "gate_step", "gate_max", "gate_exp", "gates_done"))
    gt_done, gt_hi_done, gt_lo_done = sem("gt_done"), sem("gt_hi_done"), sem("gt_lo_done")
    h_done, e_done, g_copied, hg_done, hg_hi_done, hg_lo_done = (
        sem(k) for k in ("h_done", "e_done", "g_copied", "hg_done", "hg_hi_done", "hg_lo_done"))
    y_done, y_add = sem("y_done"), sem("y_add")
    vector_waited, pool_waited = sem("f_vector_waited"), sem("f_pool_waited")

    CONSTS = 5
    UNITS = 2 * KT
    GATE_STEPS = 8
    block = ctx.enter_context(nc.Block())

    @block.sync
    def _(sp):
        def unit(k, src):
            sp.dma_start(ring[k % FFN_RING][2][:, :], src).then_inc(unit_raw[k % FFN_RING], 16)

        def do_block(b, last):
            for c in range(FFN_RING, KT):
                sp.wait_ge(h_done, b * KT + (c - 3))
                unit(c, d.w_a[c])
            if not last:
                sp.wait_ge(tt_done, b * TB + TB)
                sp.dma_start(x2_ln[:, :, :], d.x2t[b + 1]).then_inc(x2_ln_in, 16)
            for c in range(FFN_RING):
                sp.wait_ge(h_done, b * KT + (c + 5))
                unit(c, d.w_b[c])
            for c in range(KT):
                sp.wait_ge(y_done, b * KT + (c + 1))
                if c < FFN_RING:
                    unit(c, d.w_b[c + FFN_RING])
                elif not last:
                    unit(c, d.w_a[c - FFN_RING])
                sp.wait_ge(y_add, b * KT + (KT + c + 1))
                sp.dma_start(d.y_t[b, :, c, :], x2_res[:, c, :]).then_inc(y_out, 16)
            sp.wait_ge(y_out, b * (16 * KT) + 16 * KT)
            if not last:
                sp.dma_start(x2_res[:, :, :], d.x2t[b + 1]).then_inc(x2_res_in, 16)

        with sp.Fori(0, BLOCKS - 1) as b:
            do_block(b, last=False)
        do_block(BLOCKS - 1, last=True)

    @block.tensor
    def _(pe):
        def token_rows(b, t):
            if t == 0:
                pe.wait_ge(x2_ln_in, b * 16 + 16)
            if t >= 2:
                pe.wait_ge(row_norm, b * TB + (t - 1))
            for kt in range(KT):
                bank = prep_banks[2 * (t % 2) + kt // 4]
                done = nc.tensor.transpose(bank[:, (kt % 4) * P:(kt % 4) * P + P], x2_ln[:, kt, t * S:t * S + S], ident[:, :])
            done.then_inc(tt_done, 1)

        def hidden_columns(b, kts):
            for kt in kts:
                if kt == 0:
                    pe.wait_ge(row_norm, b * TB + TB)
                if kt >= 4:
                    pe.wait_ge(xn_lo_done, b * KT + (kt - 3))
                for t in range(TB):
                    done = nc.tensor.transpose(prep_banks[kt % 4][:, t * S:t * S + S], rows[:, t, kt * P:kt * P + P], ident[:, :])
                done.then_inc(xt_done, 1)

        def times_xn(bank, w, done_sem, b=None, halfway=None):
            for kt in range(KT):
                if halfway is not None and kt == KT // 2:
                    halfway()
                if b is not None:
                    pe.wait_ge(xn_lo_done, b * KT + (kt + 1))
                done = split_product(nc, bank[:, :], [(w[0][:, kt, :], w[1][:, kt, :], xn_hi[:, kt, :], xn_lo[:, kt, :])],
                                     kt == 0, kt == KT - 1)
            done.then_inc(done_sem, 1)

        def w_ready(b, k):
            pe.wait_ge(unit_lo, b * UNITS + (k + 1))
            return [w[:, :].rearrange("p (k o) -> p k o", k=KT) for w in ring[k % FFN_RING][:2]]

        def ranks(b, c, halfway=None):
            w = w_ready(b, c)
            if c < 2:
                pe.wait_ge(y_add, b * KT + (KT - 1 + c))
            if c >= 4:
                pe.wait_ge(hg_done, b * KT + (c - 3))
            times_xn(bank_h[c % 4], w, h_done, halfway=halfway)

        def gates_of_ranks(b, c):
            if c == 0:
                pe.wait_ge(gt_lo_done, b + 1)
            if c >= 2:
                pe.wait_ge(g_copied, b * KT + (c - 1))
            nc.tensor.matmul(bank_e[c % 2][:, :], expand[:, c, :], gt_hi[:, :], start=True, stop=False)
            nc.tensor.matmul(bank_e[c % 2][:, :], expand[:, c, :], gt_lo[:, :], start=False, stop=True).then_inc(e_done, 1)

        def output(b, o):
            w = w_ready(b, KT + o)
            if o >= 2:
                pe.wait_ge(y_add, b * KT + (KT + o - 1))
            else:
                pe.wait_ge(hg_done, b * KT + (5 + o))
            for c in range(KT):
                if o == 0:
                    pe.wait_ge(hg_lo_done, b * KT + (c + 1))
                done = split_product(nc, bank_h[o % 2][:, :], [(w[0][:, c, :], w[1][:, c, :], hg_hi[:, c, :], hg_lo[:, c, :])],
                                     c == 0, c == KT - 1)
            done.then_inc(y_done, 1)

        def do_block(b, last):
            times_xn(bank_h[3], (wr_hi, wr_lo), r_done, b)
            ranks(b, 0)
            pe.wait_ge(sct_copied, b + 1)
            for t in range(TB):
                done = nc.tensor.transpose(bank_x[0][:, t * P:t * P + P], sct[:, t, :], ident[:, :])
            done.then_inc(st_done, 1)
            ranks(b, 1)
            ranks(b, 2)
            pe.wait_ge(gates_done, b + 1)
            for t in range(TB):
                done = nc.tensor.transpose(bank_x[1][:, t * S:t * S + S], gates[:, t, :], ident[:, :])
            done.then_inc(gt_done, 1)

            def first_gates():
                gates_of_ranks(b, 0)
                gates_of_ranks(b, 1)

            ranks(b, 3, first_gates)
            for c in range(4, KT):
                ranks(b, c)
                if c < KT - 1:
                    gates_of_ranks(b, 2 * c - 6)
                    gates_of_ranks(b, 2 * c - 5)
            output(b, 0)
            if last:
                for o in range(1, KT):
                    output(b, o)
                return
            token_rows(b + 1, 0)
            token_rows(b + 1, 1)
            output(b, 1)
            output(b, 2)
            token_rows(b + 1, 2)
            token_rows(b + 1, 3)
            output(b, 3)
            output(b, 4)
            hidden_columns(b + 1, range(0, 4))
            output(b, 5)
            hidden_columns(b + 1, range(4, 8))
            output(b, 6)
            output(b, 7)

        pe.wait_ge(const_in, 16 * CONSTS)
        for t in range(TB):
            token_rows(0, t)
        hidden_columns(0, range(KT))
        pe.wait_ge(router_lo, 1)
        with pe.Fori(0, BLOCKS - 1) as b:
            do_block(b, last=False)
        do_block(BLOCKS - 1, last=True)

    @block.scalar
    def _(act):
        def split(b, k):
            act.wait_ge(unit_raw[k % FFN_RING], b * (16 * UNITS // FFN_RING) + 16 * (k // FFN_RING + 1))
            nc.scalar.copy(ring[k % FFN_RING][0][:, :], ring[k % FFN_RING][2][:, :]).then_inc(unit_hi, 1)

        def row_seeds(b, t):
            act.wait_ge(row_aggr, b * TB + (t + 1))
            nc.scalar.activation(ln[:, t:t + 1], mv[:, t, 1:2], ACT.Ln, bias=eps[:, :]).then_inc(row_ln, 1)
            act.wait_ge(row_ln, b * TB + (t + 1))
            nc.scalar.activation(seed[:, t:t + 1], ln[:, t:t + 1], ACT.Exp, scale=-0.5).then_inc(row_seed, 1)

        def columns_high(b, kts):
            for kt in kts:
                act.wait_ge(xt_done, b * KT + (kt + 1))
                nc.scalar.copy(xn_hi[:, kt, :], prep_banks[kt % 4][:, :]).then_inc(xn_hi_done, 1)

        def gates_copied(b, c):
            act.wait_ge(e_done, b * KT + (c + 1))
            nc.scalar.copy(g_rep[c % 2][:, :], bank_e[c % 2][:, :]).then_inc(g_copied, 1)

        def gated_high(b, c):
            act.wait_ge(hg_done, b * KT + (c + 1))
            nc.scalar.copy(hg_hi[:, c, :], hg[c % 2][:, :]).then_inc(hg_hi_done, 1)

        def do_block(b, last):
            act.wait_ge(r_done, b + 1)
            nc.scalar.copy(sct[:, :, :], bank_h[3][:, :].rearrange("p (t q) -> p t q", q=S)).then_inc(sct_copied, 1)
            split(b, 2)
            split(b, 3)
            act.wait_ge(gate_max, b + 1)
            for t in range(TB):
                done = nc.scalar.activation(ex[:, t, :], sc[:, t, :], ACT.Exp, bias=g_nmax[:, t:t + 1])
            done.then_inc(gate_exp, 1)
            act.wait_ge(gt_done, b + 1)
            nc.scalar.copy(gt_hi[:, :], bank_x[1][:, :]).then_inc(gt_hi_done, 1)
            split(b, 4)
            gates_copied(b, 0)
            for c in range(1, KT):
                gates_copied(b, c)
                gated_high(b, c - 1)
                if c < 5:
                    split(b, c + 4)
            split(b, 9)
            gated_high(b, 7)
            split(b, 10)
            split(b, 11)
            if last:
                for k in range(12, UNITS):
                    split(b, k)
                return
            row_seeds(b + 1, 0)
            row_seeds(b + 1, 1)
            split(b, 12)
            split(b, 13)
            row_seeds(b + 1, 2)
            row_seeds(b + 1, 3)
            split(b, 14)
            split(b, 15)
            columns_high(b + 1, range(0, 4))
            split(b, 16)
            columns_high(b + 1, range(4, 8))
            split(b, 17)

        act.wait_ge(const_in, 16 * CONSTS)
        nc.scalar.activation(tg[:, :], g_in[:, :], ACT.Tanh).then_inc(gate_tanh, 1)
        act.preload_act_table_set("natural_log_exp_and_others")
        for t in range(TB):
            row_seeds(0, t)
        nc.scalar.copy(wr_hi[:, :, :], wr_raw[:, :, :]).then_inc(router_hi, 1)
        nc.scalar.copy(expand[:, :, :], expand_in[:, :, :]).then_inc(router_hi, 1)
        split(0, 0)
        columns_high(0, range(KT))
        split(0, 1)
        with act.Fori(0, BLOCKS - 1) as b:
            do_block(b, last=False)
        do_block(BLOCKS - 1, last=True)

    @block.vector
    def _(dve):
        def low(out, whole, hi):
            return nc.vector.tensor_tensor(out, whole, hi.bitcast(FP32), ALU.subtract)

        def alone():
            dve.sem_inc(vector_waited, 1)

        def split(b, k):
            hi, lo, raw = ring[k % FFN_RING]
            dve.wait_ge(unit_hi, b * UNITS + (k + 1))
            low(lo[:, :], raw[:, :], hi[:, :]).then_inc(unit_lo, 1)

        def row_statistics(b, t):
            dve.wait_ge(tt_done, b * TB + (t + 1))
            for i in range(2):
                done = nc.vector.bn_stats(stats[:, t, i, :], prep_banks[2 * (t % 2) + i][:, :])
            done.then_inc(row_stats, 1)
            dve.wait_ge(row_stats, b * TB + (t + 1))
            alone()
            nc.vector.bn_aggr(mv[:, t, :], stats[:, t, :, :].rearrange("p i s -> p (i s)")).then_inc(row_aggr, 1)

        def normalise_rows(b, t):
            dve.wait_ge(rstd_step, b * (5 * TB) + 5 * (t + 1))
            for i in range(2):
                done = nc.vector.tensor_scalar(rows[:, t, i * 512:i * 512 + 512], prep_banks[2 * (t % 2) + i][:, :],
                                               mv[:, t, 0:1], rstd[:, t:t + 1], ALU.subtract, ALU.mult)
            done.then_inc(row_norm, 1)

        def columns_low(b, kts):
            for kt in kts:
                dve.wait_ge(xn_hi_done, b * KT + (kt + 1))
                low(xn_lo[:, kt, :], prep_banks[kt % 4][:, :], xn_hi[:, kt, :]).then_inc(xn_lo_done, 1)

        def choose(b):
            dve.wait_ge(st_done, b + 1)
            step = b * GATE_STEPS
            nc.vector.tensor_copy(sc[:, :, :], bank_x[0][:, :].rearrange("p (t e) -> p t e", e=P)[:, :, 0:EXPERTS]).then_inc(gate_step, 1)
            dve.wait_ge(gate_step, step + 1)
            alone()
            for t in range(TB):
                done = nc.vector.max(m1[:, t, :], sc[:, t, :])
            done.then_inc(gate_step, 1)
            dve.wait_ge(gate_step, step + 2)
            alone()
            nc.vector.tensor_scalar(g_nmax[:, :], m1[:, :, 0], -1.0, None, ALU.mult).then_inc(gate_max, 1)
            for t in range(TB):
                done = nc.vector.match_replace(w1[:, t, :], m1[:, t, :], sc[:, t, :], LOWEST)
            done.then_inc(gate_step, 1)
            dve.wait_ge(gate_step, step + 3)
            alone()
            for t in range(TB):
                done = nc.vector.max(m2[:, t, :], w1[:, t, :])
            done.then_inc(gate_step, 1)
            dve.wait_ge(gate_step, step + 4)
            alone()
            for t in range(TB):
                done = nc.vector.match_replace(w2[:, t, :], m2[:, t, :], w1[:, t, :], LOWEST)
            done.then_inc(gate_step, 1)
            dve.wait_ge(gate_step, step + 5)
            nc.vector.tensor_tensor(sel[:, :, :], w2[:, :, :], sc[:, :, :], ALU.not_equal).then_inc(gate_step, 1)

        def gate_softmax(b):
            step = b * GATE_STEPS
            dve.wait_ge(gate_exp, b + 1)
            dve.wait_ge(gate_step, step + 6)
            nc.vector.tensor_tensor(w1[:, :, :], ex[:, :, :], sel[:, :, :], ALU.mult).then_inc(gate_step, 1)
            dve.wait_ge(gate_step, step + 7)
            nc.vector.tensor_reduce(g_sum[:, :], w1[:, :, :], AX.X, ALU.add).then_inc(gate_step, 1)
            dve.wait_ge(gate_step, step + 8)
            nc.vector.reciprocal(g_inv[:, :], g_sum[:, :]).then_inc(gate_set, 1)
            dve.wait_ge(gate_set, b + 2)
            nc.vector.tensor_tensor(gates[:, :, 0:EXPERTS], w1[:, :, :], g_inv[:, :].unsqueeze(2).to_broadcast([P, TB, EXPERTS]),
                                    ALU.mult).then_inc(gates_done, 1)

        def gated(b, c):
            dve.wait_ge(h_done, b * KT + (c + 1))
            dve.wait_ge(g_copied, b * KT + (c + 1))
            nc.vector.tensor_tensor(hg[c % 2][:, :], bank_h[c % 4][:, :], g_rep[c % 2][:, :], ALU.mult).then_inc(hg_done, 1)
            dve.wait_ge(hg_hi_done, b * KT + (c + 1))
            low(hg_lo[:, c, :], hg[c % 2][:, :], hg_hi[:, c, :]).then_inc(hg_lo_done, 1)

        def add_output(b, o):
            dve.wait_ge(y_done, b * KT + (o + 1))
            if o == 0:
                dve.wait_ge(x2_res_in, b * 16 + 16)
            nc.vector.scalar_tensor_tensor(x2_res[:, o, :], bank_h[o % 2][:, :], tg2[:, :], x2_res[:, o, :],
                                           ALU.mult, ALU.add).then_inc(y_add, 1)

        def do_block(b, last):
            split(b, 2)
            choose(b)
            split(b, 3)
            gate_softmax(b)
            dve.wait_ge(gt_hi_done, b + 1)
            low(gt_lo[:, :], bank_x[1][:, :], gt_hi[:, :]).then_inc(gt_lo_done, 1)
            split(b, 4)
            for c in range(KT - 1):
                gated(b, c)
                if c < 4:
                    split(b, c + 5)
            split(b, 9)
            gated(b, 7)
            split(b, 10)
            split(b, 11)
            add_output(b, 0)
            if last:
                for o in range(1, KT):
                    if o < 5:
                        split(b, 11 + o)
                    add_output(b, o)
                return
            row_statistics(b + 1, 0)
            row_statistics(b + 1, 1)
            normalise_rows(b + 1, 0)
            normalise_rows(b + 1, 1)
            add_output(b, 1)
            split(b, 12)
            split(b, 13)
            add_output(b, 2)
            row_statistics(b + 1, 2)
            row_statistics(b + 1, 3)
            normalise_rows(b + 1, 2)
            normalise_rows(b + 1, 3)
            split(b, 14)
            add_output(b, 3)
            split(b, 15)
            add_output(b, 4)
            columns_low(b + 1, range(0, 4))
            split(b, 16)
            add_output(b, 5)
            columns_low(b + 1, range(4, 8))
            split(b, 17)
            add_output(b, 6)
            add_output(b, 7)

        dve.wait_ge(gate_tanh, 1)
        nc.vector.tensor_scalar(tg2[:, :], tg[:, :], ALPHA_OVER_RANK, None, ALU.mult).then_inc(gate_set, 1)
        dve.wait_ge(gate_set, 1)
        nc.vector.memset(gates[:, :, EXPERTS:], 0.0).then_inc(y_add, KT)
        row_statistics(0, 0)
        row_statistics(0, 1)
        normalise_rows(0, 0)
        normalise_rows(0, 1)
        row_statistics(0, 2)
        row_statistics(0, 3)
        normalise_rows(0, 2)
        normalise_rows(0, 3)
        dve.wait_ge(router_hi, 2)
        low(wr_lo[:, :, :], wr_raw[:, :, :], wr_hi[:, :, :]).then_inc(router_lo, 1)
        split(0, 0)
        columns_low(0, range(KT))
        split(0, 1)
        with dve.Fori(0, BLOCKS - 1) as b:
            do_block(b, last=False)
        do_block(BLOCKS - 1, last=True)

    @block.gpsimd
    def _(pool):
        def alone():
            pool.sem_inc(pool_waited, 1)

        def newton(b, t):
            after = b * (5 * TB) + 5 * (t + 1)
            v, y, z = nv[:, t:t + 1], seed[:, t:t + 1], nt[:, t:t + 1]
            pool.wait_ge(row_seed, b * TB + (t + 1))
            alone()
            nc.gpsimd.tensor_scalar(v, mv[:, t, 1:2], EPS, None, ALU.add).then_inc(rstd_step, 1)
            nc.gpsimd.tensor_tensor(z, y, y, ALU.mult).then_inc(rstd_step, 1)
            pool.wait_ge(rstd_step, after - 3)
            nc.gpsimd.tensor_tensor(z, z, v, ALU.mult).then_inc(rstd_step, 1)
            pool.wait_ge(rstd_step, after - 2)
            alone()
            nc.gpsimd.tensor_scalar(z, z, -0.5, 1.5, ALU.mult, ALU.add).then_inc(rstd_step, 1)
            pool.wait_ge(rstd_step, after - 1)
            nc.gpsimd.tensor_tensor(rstd[:, t:t + 1], z, y, ALU.mult).then_inc(rstd_step, 1)

        with pool.Fori(0, BLOCKS) as b:
            for t in range(TB):
                newton(b, t)


def build(nc, d):
    with ExitStack() as ctx:
        psum = [ctx.enter_context(nc.psum_tensor(f"bank{i}", [P, 512], FP32)) for i in range(8)]
        early = Early(nc, lambda name: ctx.enter_context(nc.semaphore(name)))
        for phase in (attention_phase, ffn_phase):
            with ExitStack() as part:
                phase(nc, part, lambda name: part.enter_context(nc.semaphore(name)), psum, d, early)


def lay_out(i):
    import numpy as np

    x, c = i["x"].reshape(BLOCKS, TOK, HIDDEN), i["ctx_4096"].reshape(BLOCKS, TOK, HIDDEN)

    def columns(a):
        return a.transpose(0, 2, 1).reshape(BLOCKS, KT, P, TOK).transpose(0, 2, 1, 3)

    def by_slice(w, outs):
        return w.reshape(-1, outs, KT, P).transpose(0, 3, 2, 1)

    wk, wv = by_slice(i["L0_xattn_k_proj_w"], P), by_slice(i["L0_xattn_v_proj_w"], P)
    kv = np.concatenate([wk, wv], axis=3).reshape(GROUPS, P, 2, UNIT).transpose(0, 2, 1, 3)
    o = i["L0_xattn_o_proj_w"].reshape(KT // 2, 2, P, GROUPS, GH, HEAD_DIM).transpose(3, 0, 5, 1, 4, 2)
    b = i["L0_ffn_B"].transpose(0, 2, 1).reshape(KT, P, KT, P).transpose(2, 1, 0, 3)
    wr = np.concatenate([i["L0_ffn_Wr"], np.zeros((P - EXPERTS, HIDDEN), np.float32)])
    rank_of = np.zeros((P, KT, P), np.float32)
    for j in range(LORA):
        rank_of[j // RANK, j // P, j % P] = 1.0
    out = {
        "x_rows": x.reshape(BLOCKS, TB, P, HIDDEN).transpose(0, 2, 1, 3),
        "x_t": columns(x), "ctx_t": columns(c),
        "w_kv": kv, "w_q": by_slice(i["L0_xattn_q_proj_w"], P).reshape(GROUPS, GH, P, UNIT),
        "w_o": o.reshape(GROUPS, KT // 2, P, UNIT),
        "mask": i["mask_1x1xSxS2_ff0"].reshape(S, S),
        "norm_w": np.stack([i["L0_xattn_q_norm_w"], i["L0_xattn_k_norm_w"]], axis=1),
        "g_x": np.broadcast_to(i["g_xattn"].reshape(1, 1), (P, 1)),
        "g_f": np.broadcast_to(i["g_ffn"].reshape(1, 1), (P, 1)),
        "ident": np.eye(P, dtype=np.float32), "eps": np.full((P, 1), EPS, np.float32),
        "w_a": by_slice(i["L0_ffn_A"].reshape(LORA, HIDDEN), P).reshape(KT, P, UNIT),
        "w_b": b.reshape(KT, P, UNIT), "w_r": by_slice(wr, P).reshape(P, UNIT),
        "expand": rank_of,
    }
    return {k: np.ascontiguousarray(v) for k, v in out.items()}


class Declared:

    def __init__(self, nc, arrays):
        def arg(name):
            return nc.dram_tensor(f"in_{name}", arrays[name].shape, FP32, kind="ExternalInput").ap()

        self.x_rows = arg("x_rows")
        self.x_t = arg("x_t")
        self.ctx_t = arg("ctx_t")
        self.w_kv = arg("w_kv")
        self.w_q = arg("w_q")
        self.w_o = arg("w_o")
        self.mask = arg("mask")
        self.norm_w = arg("norm_w")
        self.g_x = arg("g_x")
        self.g_f = arg("g_f")
        self.ident = arg("ident")
        self.eps = arg("eps")
        self.w_a = arg("w_a")
        self.w_b = arg("w_b")
        self.w_r = arg("w_r")
        self.expand = arg("expand")
        self.x2t = nc.dram_tensor("x2t", (BLOCKS, P, KT, TOK), FP32).ap()
        self.y_t = nc.dram_tensor("out_y", (BLOCKS, P, KT, TOK), FP32, kind="ExternalOutput").ap()


def kernel(**inputs):
    import numpy as np
    from concourse.bacc import Bacc
    from concourse.bass_utils import run_bass_kernel_spmd

    arrays = lay_out({k: np.asarray(v) for k, v in inputs.items()})
    nc = Bacc("TRN2", target_bir_lowering=False, num_devices=1)
    build(nc, Declared(nc, arrays))
    r = run_bass_kernel_spmd(nc, [{f"in_{k}": v for k, v in arrays.items()}], core_ids=[0])
    y = r.results[0]["out_y"]
    return y.transpose(0, 3, 2, 1).reshape(BATCHES, S, HIDDEN)
```
